# Optimizing a Trainium2 kernel written in Bass

```python
import numpy as np
import jax
import jax.numpy as jnp

def _softmax(x, axis=-1):
    return jax.nn.softmax(x, axis=axis)

def _gelu(x):
    return jax.nn.gelu(x, approximate=True)

def _silu(x):
    return jax.nn.silu(x)

def _sigmoid(x):
    return jax.nn.sigmoid(x)

def _layernorm(x, axis=-1, eps=1e-05):
    m = jnp.mean(x, axis=axis, keepdims=True)
    v = jnp.var(x, axis=axis, keepdims=True)
    return (x - m) / jnp.sqrt(v + eps)

def _scatter_add(tgt, idx, src, axis=0):
    return tgt.at[idx].add(src)

def _segment_sum(src, seg, n):
    return jax.ops.segment_sum(src, seg, n)
kernel_name = 'mk_adaln_d1_jaxref_r8_1b7f66'

def setup_inputs(seed: int=0):
    np.random.seed(seed)
    _w = jnp.asarray

    def _L0_attn_setup():
        import jax, jax.numpy as jnp
        import numpy as np
        B, T, C = (2, 256, 128)
        DIM, H = (128, 16)
        HD = DIM // H
        key = jax.random.key(seed)
        ks = jax.random.split(key, 6)
        s_in = 1.0 / np.sqrt(C)
        s_proj = 1.0 / np.sqrt(DIM)
        return {'x': jax.random.normal(ks[0], (B, T, C), dtype=jnp.float32), 'Wqkv': jax.random.normal(ks[1], (C, 3 * DIM), dtype=jnp.float32) * s_in, 'bqkv': jnp.zeros((3 * DIM,), dtype=jnp.float32), 'r_sigma': jnp.float32(0.1), 'Wproj': jax.random.normal(ks[2], (DIM, C), dtype=jnp.float32) * s_proj, 'bproj': jnp.zeros((C,), dtype=jnp.float32)}
    _L0_attn_in = _L0_attn_setup()

    def _L0_ffn_setup():
        import jax, jax.numpy as jnp
        import numpy as np
        B, T, D_IN, D_OUT = (4, 256, 128, 128)
        N_EXPERTS, N_ACTIVE = (8, 2)
        key = jax.random.key(seed)
        k1, k2, k3, k4, k5 = jax.random.split(key, 5)
        s_in = 1.0 / np.sqrt(D_IN)
        x = jax.random.normal(k1, (B, T, D_IN), dtype=jnp.float32)
        w_router = jax.random.uniform(k2, (N_EXPERTS, D_IN), jnp.float32, -s_in, s_in)
        b_router = jax.random.uniform(k3, (N_EXPERTS,), jnp.float32, -s_in, s_in)
        w_experts = jax.random.uniform(k4, (N_EXPERTS, D_OUT, D_IN), jnp.float32, -s_in, s_in)
        b_experts = jax.random.uniform(k5, (N_EXPERTS, D_OUT), jnp.float32, -s_in, s_in)
        return {'x': x, 'w_router': w_router, 'b_router': b_router, 'w_experts': w_experts, 'b_experts': b_experts}
    _L0_ffn_in = _L0_ffn_setup()
    _L0_c = _w((lambda *s: np.random.randn(*s).astype(np.float32) * 0.05)(16, 128))
    _L0_wmod = _w((lambda *s: np.random.randn(*s).astype(np.float32) * 0.05)(128, 6 * 128) * 128 ** (-0.5))
    _d = {'L0_attn_x': _L0_attn_in['x'], 'L0_attn_Wqkv': _L0_attn_in['Wqkv'], 'L0_attn_bqkv': _L0_attn_in['bqkv'], 'L0_attn_r_sigma': _L0_attn_in['r_sigma'], 'L0_attn_Wproj': _L0_attn_in['Wproj'], 'L0_attn_bproj': _L0_attn_in['bproj'], 'L0_ffn_w_router': _L0_ffn_in['w_router'], 'L0_ffn_b_router': _L0_ffn_in['b_router'], 'L0_ffn_w_experts': _L0_ffn_in['w_experts'], 'L0_ffn_b_experts': _L0_ffn_in['b_experts'], 'L0_c': _L0_c, 'L0_wmod': _L0_wmod}
    _x0 = _d['L0_attn_x']
    _d['L0_attn_x'] = jax.random.normal(jax.random.fold_in(jax.random.key(seed), 1), (16, 256, 128), dtype=_x0.dtype)
    del _x0
    return _d

def reference(L0_attn_x, L0_attn_Wqkv, L0_attn_bqkv, L0_attn_r_sigma, L0_attn_Wproj, L0_attn_bproj, L0_ffn_w_router, L0_ffn_b_router, L0_ffn_w_experts, L0_ffn_b_experts, L0_c, L0_wmod):

    def _L0_attn_ref(x, Wqkv, bqkv, r_sigma, Wproj, bproj):
        import jax, jax.numpy as jnp
        import numpy as np
        B, T, C = (2, 256, 128)
        DIM, H = (128, 16)
        HD = DIM // H
        b, t, c = x.shape
        qkv = x @ Wqkv + bqkv
        qkv = qkv.reshape(b, t, 3, H, HD).transpose(2, 0, 3, 1, 4)
        q, k, v = (qkv[0], qkv[1], qkv[2])
        qn = jnp.sum(q * q, axis=-1)
        kn = jnp.sum(k * k, axis=-1)
        dot = jnp.einsum('bhid,bhjd->bhij', k, q)
        dist2 = kn[..., :, None] + qn[..., None, :] - 2.0 * dot
        Kmat = jnp.exp(-dist2 * r_sigma)
        out = jnp.einsum('bhij,bhjd->bhid', Kmat, v)
        out = out.transpose(0, 2, 1, 3).reshape(b, t, DIM)
        return out @ Wproj + bproj

    def _L0_ffn_ref(x, w_router, b_router, w_experts, b_experts):
        import jax, jax.numpy as jnp
        import numpy as np
        B, T, D_IN, D_OUT = (4, 256, 128, 128)
        N_EXPERTS, N_ACTIVE = (8, 2)
        gamma = jax.nn.softmax(jnp.einsum('btd,ed->bte', x, w_router) + b_router, axis=-1)
        _, expert_ids = jax.lax.top_k(gamma, N_ACTIVE)
        mask = (expert_ids[..., None] == jnp.arange(N_EXPERTS)).any(axis=-2)
        y_all = jnp.einsum('btd,eod->bteo', x, w_experts) + b_experts
        y = jnp.einsum('bte,bteo->bto', mask.astype(x.dtype), y_all)
        return y
    x = L0_attn_x
    mod = (_silu(L0_c) @ L0_wmod).reshape(L0_c.shape[0], 6, 1, -1)
    sa, ca, ga, sb, cb, gb = (mod[:, 0], mod[:, 1], mod[:, 2], mod[:, 3], mod[:, 4], mod[:, 5])
    ga = (2 * (ga >= 0) - 1) * jnp.maximum(jnp.abs(ga), 0.25)
    gb = (2 * (gb >= 0) - 1) * jnp.maximum(jnp.abs(gb), 0.25)
    h = _layernorm(x, axis=-1) * (1 + ca) + sa
    x = x + ga * _L0_attn_ref(h, L0_attn_Wqkv, L0_attn_bqkv, L0_attn_r_sigma, L0_attn_Wproj, L0_attn_bproj)
    h = _layernorm(x, axis=-1) * (1 + cb) + sb
    x = x + gb * _L0_ffn_ref(h, L0_ffn_w_router, L0_ffn_b_router, L0_ffn_w_experts, L0_ffn_b_experts)
    return x

_drawn_inputs = setup_inputs


def setup_inputs(seed=0):
    import zlib

    import numpy as np

    out = dict(_drawn_inputs(seed))
    spreads = {'L0_attn_bqkv': (0.0, 0.1), 'L0_attn_bproj': (0.0, 0.614)}
    factors = {'L0_ffn_b_experts': 8.0}
    for name, (base, spread) in spreads.items():
        noise = np.random.default_rng([zlib.crc32(name.encode()), seed]).standard_normal(out[name].shape)
        drawn = base * np.exp(spread * noise) if base else spread * noise
        out[name] = jnp.asarray(drawn.astype(out[name].dtype))
    for name, factor in factors.items():
        out[name] = (out[name] * factor).astype(out[name].dtype)
    return out
```

```python
from contextlib import ExitStack

import concourse.bass as bass
from concourse import mybir

F32 = mybir.dt.float32
F32R = mybir.dt.float32r
U32 = mybir.dt.uint32
ALU = mybir.AluOpType
ACT = mybir.ActivationFunctionType
AX = mybir.AxisListType

LN_EPS = 1e-5
GATE_MIN = 0.25
WARM = 20
LOOK = 5


def adaln_block(nc, x, w_qkv, b_qkv, sigma, w_proj, b_proj, w_router, b_router, w_experts, b_experts, cond, w_mod, out):
    NB, T, C = x.shape
    P = 128
    NT = T // P
    NE = w_router.shape[0]
    HD = 8
    H = C // HD
    R = 4
    G = H // R
    ROWS = P // R
    VBLK = 160
    NC = 4
    EC = NE // NC
    RB = 3 * C + NE
    NP = 4
    NQKV = 3 * C
    NW = NE * C + NE

    xv = x.rearrange("b (p t) c -> b p (t c)", t=NT)
    ov = out.rearrange("b (p t) c -> b p (t c)", t=NT)

    cb_dram = nc.dram_tensor("cb_rows", [NB, NQKV], F32).ap()
    rb_dram = nc.dram_tensor("rb_rows", [NB, RB], F32).ap()
    fb_dram = nc.dram_tensor("fb_rows", [NB, NE * C], F32).ap()

    with ExitStack() as ctx:
        def sb(name, shape, dt=F32):
            return ctx.enter_context(nc.sbuf_tensor(name, shape, dt))

        def sem(name):
            return ctx.enter_context(nc.semaphore(name))

        scores = ctx.enter_context(nc.psum_tensor("scores", [P, R, NT * T], F32))
        att_ps = ctx.enter_context(nc.psum_tensor("att_ps", [P, 512], F32))
        work = [ctx.enter_context(nc.psum_tensor(f"work{i}", [P, 512], F32)) for i in range(3)]

        x_all = sb("x_all", [P, NB, NT * C])
        cb_all = sb("cb_all", [P, NB, NQKV])
        rb_all = sb("rb_all", [P, NB, RB])
        fb_all = sb("fb_all", [2 * NE, NB, C], F32R)
        ident = sb("ident", [P, P])
        wq_hi = sb("wq_hi", [P, NQKV], F32R)
        wq_lo = sb("wq_lo", [P, NQKV], F32R)
        we_hi = sb("we_hi", [P, NW], F32R)
        we_lo = sb("we_lo", [P, NW], F32R)
        wproj_sb = sb("wproj_sb", [P, C])
        scale_col = sb("scale_col", [P, 2, NB])
        sig = sb("sig", [P, 3])
        expo = sb("expo", [P, NT])
        eps = sb("eps", [P, NT])
        slot_e = sb("slot_e", [P, NT, 2, NE])

        stats = sb("stats", [P, 2, NT, 6])
        mv = sb("mv", [P, 2, NT, 2])
        ve = sb("ve", [P, 2, NT])
        rstd = sb("rstd", [P, 2, NT])
        xn = sb("xn", [P, 2, NT * C])
        h1_hi = sb("h1_hi", [P, T], F32R)
        h1_lo = sb("h1_lo", [P, T], F32R)
        qk = sb("qk", [P, 2, NT, C])
        sq = sb("sq", [P, 2, NT, C])
        norms = sb("norms", [P, 2, NT * H])
        stk = sb("stk", [P, 2 * (NT * H * ROWS + 2)], F32R)
        st_t = sb("st_t", [P, 2, G, 2 * T], F32R)
        vpad = sb("vpad", [P, 2, NT, R, VBLK])
        probs = sb("probs", [P, NP, R, NT * T])
        o_hi = sb("o_hi", [P, T], F32R)
        o_lo = sb("o_lo", [P, T], F32R)
        wg = sb("wg", [P, C])
        wg_hi = sb("wg_hi", [P, 2, C], F32R)
        wg_lo = sb("wg_lo", [P, 2, C], F32R)
        x2n = sb("x2n", [P, 2, NT * C])
        h2_hi = sb("h2_hi", [P, 2, T], F32R)
        h2_lo = sb("h2_lo", [P, 2, T], F32R)
        logit = sb("logit", [P, NT, NE])
        top = sb("top", [P, NT, NE])
        topi = sb("topi", [P, NT, NE], U32)
        eq = sb("eq", [P, NT, 2, NE])
        mask = sb("mask", [P, 2, NT, 2, NE])
        mask_t = sb("mask_t", [2 * NE, T], F32R)
        fb_b = sb("fb_b", [2 * NE, C], F32R)
        acc = sb("acc", [P, 2, NT, C])
        gated = sb("gated", [P, NT * C])

        spare = probs[:, :, :, :].rearrange("p a r n -> p (a r n)")
        w_mod_sb = spare[:, 0:6 * C]
        wqkv_sb = sb("wqkv_sb", [P, NQKV])
        wr_sb = sb("wr_sb", [NE, C])
        we_sb = spare[:, 1024:1024 + NE * C].rearrange("p (e c) -> p e c", e=NE)
        we_t = spare[:, 2048:2048 + NW]
        c_sb = sb("c_sb", [NB, 3, C])
        s_t = sb("s_t", [P, NB])
        shift_col = sb("shift_col", [P, 2, NB])
        bq16 = sb("bq16", [NB, NQKV])
        bp16 = sb("bp16", [NB, C])
        be16 = spare[0:NB, 4096:4096 + NW]
        cb16 = sb("cb16", [NB, NQKV])
        rb16 = sb("rb16", [NB, RB])
        fb16 = sb("fb16", [NB, NW])
        g_up = sb("g_up", [NB, 2, C])
        g_down = sb("g_down", [NB, 2, C])
        fb_f32 = sb("fb_f32", [2 * NE, NB, C])
        fb_h = sb("fb_h", [2 * NE, NB, C], F32R)
        lo_rows = sb("lo_rows", [2 * NE, 1])

        ld_c = sem("ld_c")
        ld_mod = sem("ld_mod")
        ld_qkv = sem("ld_qkv")
        ld_x0 = sem("ld_x0")
        ld_bq = sem("ld_bq")
        ld_bp = sem("ld_bp")
        ld_sig = sem("ld_sig")
        rows_in = sem("rows_in")
        ld_we = sem("ld_we")
        ld_wr = sem("ld_wr")
        ld_be = sem("ld_be")
        ld_br = sem("ld_br")
        ld_proj = sem("ld_proj")
        st_cb = sem("st_cb")
        st_rb = sem("st_rb")
        st_fb = sem("st_fb")
        ld_cb0 = sem("ld_cb0")
        ld_fb = sem("ld_fb")
        stored = sem("stored")
        ident_z = sem("ident_z")
        ident_ok = sem("ident_ok")
        const_ok = sem("const_ok")
        expo_ok = sem("expo_ok")
        c_exp = sem("c_exp")
        c_den = sem("c_den")
        c_rec = sem("c_rec")
        c_silu = sem("c_silu")
        ct_ps = sem("ct_ps")
        ct_sb = sem("ct_sb")
        mod_ps = sem("mod_ps")
        gate_ps = sem("gate_ps")
        mod_sb = sem("mod_sb")
        cb_ps = sem("cb_ps")
        cb_sb = sem("cb_sb")
        sig_ok = sem("sig_ok")
        g_step = sem("g_step")
        gates_ok = sem("gates_ok")
        wq_hi_ok = sem("wq_hi_ok")
        wq_ok = sem("wq_ok")
        wet_ps = sem("wet_ps")
        wet_sb = sem("wet_sb")
        we_hi_ok = sem("we_hi_ok")
        we_ok = sem("we_ok")
        fb_ps = sem("fb_ps")
        fb_sb = sem("fb_sb")
        rb_ok = sem("rb_ok")
        fb_h_ok = sem("fb_h_ok")
        fb_ok = sem("fb_ok")
        ln1_bn = sem("ln1_bn")
        ln1_mv = sem("ln1_mv")
        ln1_ve = sem("ln1_ve")
        ln1_rstd = sem("ln1_rstd")
        xn_ok = sem("xn_ok")
        t1_ps = sem("t1_ps")
        t1_hi = sem("t1_hi")
        t1_ok = sem("t1_ok")
        qkv_ps = sem("qkv_ps")
        qk_sb = sem("qk_sb")
        sq_ok = sem("sq_ok")
        norm_ok = sem("norm_ok")
        part_hi = sem("part_hi")
        stk_ok = sem("stk_ok")
        st_ps = sem("st_ps")
        st_sb = sem("st_sb")
        qk_a = sem("qk_a")
        qk_b = sem("qk_b")
        exp_a = sem("exp_a")
        exp_b = sem("exp_b")
        pv_done = sem("pv_done")
        att_hi = sem("att_hi")
        att_ok = sem("att_ok")
        wg_f = sem("wg_f")
        wg_h = sem("wg_h")
        wg_ok = sem("wg_ok")
        xp_ok = sem("xp_ok")
        proj_ps = sem("proj_ps")
        x1_ok = sem("x1_ok")
        ln2_bn = sem("ln2_bn")
        ln2_mv = sem("ln2_mv")
        ln2_ve = sem("ln2_ve")
        ln2_rstd = sem("ln2_rstd")
        x2n_ok = sem("x2n_ok")
        h2_ps = sem("h2_ps")
        h2_hi_ok = sem("h2_hi_ok")
        h2_ok = sem("h2_ok")
        r_ps = sem("r_ps")
        logit_ok = sem("logit_ok")
        top_ok = sem("top_ok")
        topi_ok = sem("topi_ok")
        eq_ok = sem("eq_ok")
        mask_ok = sem("mask_ok")
        m_ps = sem("m_ps")
        m_sb = sem("m_sb")
        fbb_ok = sem("fbb_ok")
        b_ps = sem("b_ps")
        acc_init = sem("acc_init")
        f_ps = sem("f_ps")
        acc_step = sem("acc_step")
        gated_ok = sem("gated_ok")
        res_ok = sem("res_ok")

        stk_q = stk[:, 0:NT * H * ROWS].rearrange("p (h w) -> p h w", w=ROWS)
        stk_k = stk[:, NT * H * ROWS:2 * NT * H * ROWS].rearrange("p (h w) -> p h w", w=ROWS)
        stk_qk = stk[:, :].rearrange("p (a n) -> p a n", a=2)
        NQ = 3 * HD

        def norm_rows(i):
            return stk_qk[:, :, NQ + i:NQ + i + (NT * H - 1) * ROWS + 1:ROWS]

        block = ctx.enter_context(nc.Block())

        def has(b):
            return not isinstance(b, int) or 0 <= b < NB

        def steps(eng, step):
            for k in range(-2, 2):
                step(k, k % 2)
            with eng.Fori(1, NB // 2 - 1, 1) as i:
                for u in range(2):
                    step(2 * i + u, u)
            for k in range(NB - 2, NB + 2):
                step(k, k % 2)

        def wait_apart(eng, semaphore, value):
            eng.wait_ge(ident_ok, 1)
            eng.wait_ge(semaphore, value)

        def col(t, b):
            return t[:, bass.ds(b, 1)]

        @block.sync
        def _(sp):
            sp.dma_start(c_sb[:, 0, :], cond).then_inc(ld_c, 16)
            sp.dma_start(w_mod_sb[:, :], w_mod).then_inc(ld_mod, 16)
            sp.dma_start(x_all[:, 0:2, :], xv[0:2].rearrange("b p n -> p b n")).then_inc(ld_x0, 16)
            sp.dma_start(sig[:, 0:1], sigma.partition_broadcast(P)).then_inc(ld_sig, 16)
            sp.dma_start(we_sb[:, :, :], w_experts.rearrange("e o d -> o e d")).then_inc(ld_we, 16)
            sp.dma_start(wr_sb[:, :], w_router).then_inc(ld_wr, 16)
            sp.dma_start(be16[:, 0:NE * C], b_experts.rearrange("e o -> (e o)").partition_broadcast(NB)).then_inc(ld_be, 16)
            sp.dma_start(be16[:, NE * C:NW], b_router.partition_broadcast(NB)).then_inc(ld_br, 16)
            sp.wait_ge(cb_sb, 1)
            sp.dma_start(cb_dram, cb16[:, :]).then_inc(st_cb, 16)
            sp.wait_ge(st_cb, 16)
            sp.dma_start(cb_all[:, 0:2, :], cb_dram[0:2].partition_broadcast(P)).then_inc(ld_cb0, 16)
            sp.wait_ge(fb_sb, 1)
            sp.dma_start(fb_dram, fb16[:, 0:NE * C]).then_inc(st_fb, 16)
            sp.wait_ge(rb_ok, 1)
            sp.dma_start(rb_dram, rb16[:, :]).then_inc(st_rb, 16)
            sp.wait_ge(st_fb, 16)
            for half in range(2):
                sp.dma_start(fb_f32[half * NE:(half + 1) * NE, :, :],
                             fb_dram.rearrange("b (e o) -> e b o", e=NE)).then_inc(ld_fb, 16)
            sp.wait_ge(st_rb, 16)
            sp.dma_start(rb_all[:, 0:LOOK, :], rb_dram[0:LOOK].partition_broadcast(P)).then_inc(rows_in, 16)
            sp.dma_start(cb_all[:, 2:LOOK, :], cb_dram[2:LOOK].partition_broadcast(P)).then_inc(rows_in, 16)

            def store(b):
                sp.wait_ge(res_ok, b + 1)
                sp.dma_start(ov[b], x_all[:, b, :]).then_inc(stored, 16)

            with sp.Fori(0, NB - LOOK, 1) as b:
                store(b)
                sp.wait_ge(rows_in, 48 * b + 48)
                n = b + LOOK
                sp.dma_start(x_all[:, n, :], xv[n]).then_inc(rows_in, 16)
                sp.dma_start(cb_all[:, n, :], cb_dram[n].partition_broadcast(P)).then_inc(rows_in, 16)
                sp.dma_start(rb_all[:, n, :], rb_dram[n].partition_broadcast(P)).then_inc(rows_in, 16)
            with sp.Fori(NB - LOOK, NB, 1) as b:
                store(b)
            sp.wait_ge(stored, 16 * NB)

        @block.gpsimd
        def _(pool):
            nc.gpsimd.memset(ident[:, :], 0.0).then_inc(ident_z, 1)
            nc.gpsimd.memset(lo_rows[:, :], 0.0).then_inc(ident_z, 1)
            pool.wait_ge(ident_z, 2)
            nc.gpsimd.affine_select(out=ident[:, :], in_=ident[:, :], compare_op=ALU.not_equal, fill=1.0, base=0,
                                    pattern=[[-1, P]], channel_multiplier=1).then_inc(ident_ok, 1)
            nc.gpsimd.affine_select(out=lo_rows[:, :], in_=lo_rows[:, :], compare_op=ALU.is_ge, fill=-1.0, base=NE - 1,
                                    pattern=[[0, 1]], channel_multiplier=-1).then_inc(const_ok, 1)
            nc.gpsimd.memset(expo[:, :], -0.5).then_inc(expo_ok, 1)
            nc.gpsimd.memset(eps[:, :], LN_EPS).then_inc(expo_ok, 1)
            nc.gpsimd.memset(stk[:, :].bitcast(F32), 0.0).then_inc(const_ok, 1)
            nc.gpsimd.memset(vpad[:, :, :, :, :].rearrange("p a t r n -> p (a t r n)"), 0.0).then_inc(const_ok, 1)
            nc.gpsimd.iota(slot_e[:, :, :, :], [[0, NT], [0, 2], [1, NE]], base=0, channel_multiplier=0,
                           allow_small_or_imprecise_dtypes=True).then_inc(const_ok, 1)
            pool.wait_ge(const_ok, 4)
            nc.gpsimd.memset(stk_q[:, :, NQ + 2:NQ + 4].bitcast(F32), 1.0).then_inc(const_ok, 1)
            nc.gpsimd.memset(stk_k[:, :, NQ:NQ + 2].bitcast(F32), 1.0).then_inc(const_ok, 1)

            def rsqrt(n, b, bn, ve_ok, done):
                wait_apart(pool, bn, b + 1)
                nc.gpsimd.tensor_tensor(ve[:, n, :], mv[:, n, :, 1], eps[:, :], ALU.add).then_inc(ve_ok, 1)
                wait_apart(pool, ve_ok, b + 1)
                nc.gpsimd.tensor_tensor(rstd[:, n, :], ve[:, n, :], expo[:, :], ALU.pow).then_inc(done, 1)

            def step(k, par):
                if has(k - 2):
                    b = k - 2
                    if not isinstance(k, int) or k > 2:
                        wait_apart(pool, b_ps, b)
                    else:
                        pool.wait_ge(fb_ok, 1)
                    nc.gpsimd.tensor_copy(fb_b[:, :], fb_all[:, b, :].bitcast(F32)).then_inc(fbb_ok, 1)
                if has(k - 1):
                    b, q = k - 1, (par + 1) % 2
                    if isinstance(k, int) and k == 1:
                        pool.wait_ge(rows_in, 48)
                        pool.wait_ge(ld_proj, 16 * R)
                    if not isinstance(k, int) or k > 1:
                        wait_apart(pool, wg_ok, b)
                    nc.gpsimd.tensor_tensor(wg[:, :], wproj_sb[:, :], rb_all[:, b, 0:C], ALU.mult).then_inc(wg_f, 1)
                    wait_apart(pool, wg_f, b + 1)
                    nc.gpsimd.tensor_copy(wg_hi[:, q, :], wg[:, :]).then_inc(wg_h, 1)
                    wait_apart(pool, wg_h, b + 1)
                    nc.gpsimd.tensor_tensor(wg_lo[:, q, :], wg[:, :], wg_hi[:, q, :].bitcast(F32), ALU.subtract).then_inc(wg_ok, 1)
                    for t in range(NT):
                        xs = x_all[:, b, t * C:(t + 1) * C]
                        i = nc.gpsimd.tensor_tensor(xs, xs, rb_all[:, b, C:2 * C], ALU.add)
                    i.then_inc(xp_ok, 1)
                if has(k + 1):
                    b = k + 1
                    pool.wait_ge(qk_sb, 2 * b + 2)
                    nc.gpsimd.tensor_tensor(sq[:, :, :, :].rearrange("p a t c -> p (a t c)"), qk[:, :, :, :].rearrange("p a t c -> p (a t c)"),
                                            qk[:, :, :, :].rearrange("p a t c -> p (a t c)"), ALU.mult).then_inc(sq_ok, 1)
                if has(k + 2):
                    rsqrt(0, k + 2, ln1_mv, ln1_ve, ln1_rstd)
                if has(k - 1):
                    rsqrt(1, k - 1, ln2_mv, ln2_ve, ln2_rstd)
                if has(k - 2):
                    b, q = k - 2, par
                    wait_apart(pool, acc_step, NE * NT * (b + 1))
                    for t in range(NT):
                        i = nc.gpsimd.tensor_tensor(gated[:, t * C:(t + 1) * C], acc[:, q, t, :], rb_all[:, b, 2 * C:3 * C], ALU.mult)
                    i.then_inc(gated_ok, 1)
                    wait_apart(pool, gated_ok, b + 1)
                    nc.gpsimd.tensor_tensor(x_all[:, b, :], x_all[:, b, :], gated[:, :], ALU.add).then_inc(res_ok, 1)

            steps(pool, step)

        @block.scalar
        def _(act):
            act.dma_start(wqkv_sb[:, :], w_qkv).then_inc(ld_qkv, 16)
            act.dma_start(bq16[:, :], b_qkv.partition_broadcast(NB)).then_inc(ld_bq, 16)
            act.dma_start(bp16[:, :], b_proj.partition_broadcast(NB)).then_inc(ld_bp, 16)
            for r in range(R):
                act.dma_start(wproj_sb[r * ROWS:(r + 1) * ROWS, :],
                              w_proj.rearrange("(g r d) n -> r g d n", g=G, r=R)[r]).then_inc(ld_proj, 16)
            act.dma_start(x_all[:, 2:LOOK, :], xv[2:LOOK].rearrange("b p n -> p b n")).then_inc(rows_in, 16)
            act.wait_ge(ld_c, 16)
            nc.scalar.activation(c_sb[:, 1, :], c_sb[:, 0, :], ACT.Exp, scale=-1.0).then_inc(c_exp, 1)
            act.wait_ge(ld_qkv, 16)
            nc.scalar.copy(wq_hi[:, :], wqkv_sb[:, :]).then_inc(wq_hi_ok, 1)

            def expert_weights():
                act.wait_ge(wet_ps, 1)
                nc.scalar.copy(we_t[:, 0:2 * 512], scores[:, 0:2, :].rearrange("p r n -> p (r n)"))
                nc.scalar.copy(we_t[:, NE * C:NW], scores[:, 2, 0:NE]).then_inc(wet_sb, 1)
                act.wait_ge(wet_sb, 1)
                nc.scalar.copy(we_hi[:, :], we_t[:, :]).then_inc(we_hi_ok, 1)

            def exp(k, g, half):
                n = 4 * k + g
                done = (exp_a, exp_b)[half]
                act.wait_ge((qk_a, qk_b)[half], n + 1)
                if not isinstance(n, int) or n >= NP:
                    act.wait_ge(pv_done, n - NP + 1)
                nc.scalar.activation(probs[:, g, 2 * half:2 * half + 2, :], scores[:, 2 * half:2 * half + 2, :], ACT.Exp).then_inc(done, 1)

            def stack_out(b, q, g, bank):
                act.wait_ge(st_ps, 4 * b + g + 1)
                nc.scalar.copy(st_t[:, q, g, :], work[bank][:, :]).then_inc(st_sb, 1)

            def step(k, par):
                odd = (par + 1) % 2
                if has(k):
                    exp(k, 0, 0)
                    stack_out(k, par, 2, 0)
                    exp(k, 0, 1)
                    stack_out(k, par, 3, 1)
                if has(k - 2):
                    act.wait_ge(h2_ps, k - 1)
                    nc.scalar.activation(h2_hi[:, par, :], work[2][:, 0:T], ACT.Identity, scale=col(scale_col[:, 1, :], k - 2)).then_inc(h2_hi_ok, 1)
                if has(k - 1):
                    act.wait_ge(pv_done, 4 * k)
                    nc.scalar.copy(o_hi[:, :], att_ps[:, 0:T]).then_inc(att_hi, 1)
                if has(k + 1):
                    act.wait_ge(t1_ps, k + 2)
                    nc.scalar.activation(h1_hi[:, :], work[0][:, 0:T], ACT.Identity, scale=col(scale_col[:, 0, :], k + 1)).then_inc(t1_hi, 1)
                if has(k):
                    exp(k, 1, 0)
                    exp(k, 1, 1)
                    exp(k, 2, 0)
                if has(k - 2):
                    act.wait_ge(m_ps, k - 1)
                    nc.scalar.copy(mask_t[:, :], work[1][0:2 * NE, T:2 * T]).then_inc(m_sb, 1)
                if has(k):
                    exp(k, 2, 1)
                if has(k - 2):
                    act.wait_ge(b_ps, k - 1)
                    nc.scalar.copy(acc[:, par, :, :].rearrange("p t c -> p (t c)"), work[2][:, 0:NT * C]).then_inc(acc_init, 1)
                if has(k):
                    exp(k, 3, 0)
                    exp(k, 3, 1)
                if isinstance(k, int) and k == -1:
                    expert_weights()
                if has(k + 1):
                    stack_out(k + 1, odd, 0, 0)
                    stack_out(k + 1, odd, 1, 1)

            steps(act, step)

        @block.vector
        def _(dve):
            v = nc.vector
            dve.wait_ge(c_exp, 1)
            v.tensor_scalar(c_sb[:, 1, :], c_sb[:, 1, :], 1.0, None, ALU.add).then_inc(c_den, 1)
            dve.wait_ge(c_den, 1)
            v.reciprocal(c_sb[:, 2, :], c_sb[:, 1, :]).then_inc(c_rec, 1)
            dve.wait_ge(c_rec, 1)
            v.tensor_tensor(c_sb[:, 1, :], c_sb[:, 0, :], c_sb[:, 2, :], ALU.mult).then_inc(c_silu, 1)
            dve.wait_ge(ct_ps, 1)
            v.tensor_copy(s_t[:, :], work[0][:, 0:NB]).then_inc(ct_sb, 1)
            dve.wait_ge(mod_ps, 1)
            mod_cols = work[1][:, 0:4 * NB].rearrange("p (m b) -> p m b", m=4)
            v.tensor_copy(shift_col[:, :, :], mod_cols[:, 0:4:2, :]).then_inc(mod_sb, 1)
            v.tensor_scalar(scale_col[:, :, :], mod_cols[:, 1:4:2, :], 1.0, None, ALU.add).then_inc(mod_sb, 1)
            dve.wait_ge(wq_hi_ok, 1)
            v.tensor_tensor(wq_lo[:, :], wqkv_sb[:, :], wq_hi[:, :].bitcast(F32), ALU.subtract).then_inc(wq_ok, 1)
            dve.wait_ge(ld_sig, 16)
            v.tensor_scalar(sig[:, 1:2], sig[:, 0:1], 2.0, None, ALU.mult).then_inc(sig_ok, 1)
            v.tensor_scalar(sig[:, 2:3], sig[:, 0:1], -1.0, None, ALU.mult).then_inc(sig_ok, 1)
            dve.wait_ge(cb_ps, 1)
            dve.wait_ge(ld_bq, 16)
            v.tensor_tensor(cb16[:, :], work[2][0:NB, 0:NQKV], bq16[:, :], ALU.add).then_inc(cb_sb, 1)
            dve.wait_ge(gate_ps, 1)
            gates = scores[0:NB, 3, 0:2 * C].rearrange("b (m c) -> b m c", m=2)
            v.tensor_scalar(g_up[:, :, :], gates, GATE_MIN, None, ALU.max).then_inc(g_step, 1)
            v.tensor_scalar(g_down[:, :, :], gates, -GATE_MIN, None, ALU.min).then_inc(g_step, 1)
            dve.wait_ge(g_step, 2)
            v.scalar_tensor_tensor(g_up[:, :, :], gates, 0.0, g_up[:, :, :], ALU.is_ge, ALU.mult).then_inc(g_step, 1)
            v.scalar_tensor_tensor(g_down[:, :, :], gates, 0.0, g_down[:, :, :], ALU.is_lt, ALU.mult).then_inc(g_step, 1)
            dve.wait_ge(g_step, 4)
            dve.wait_ge(ld_bp, 16)
            v.tensor_tensor(rb16[:, 0:C], g_up[:, 0, :], g_down[:, 0, :], ALU.add).then_inc(g_step, 1)
            v.tensor_tensor(rb16[:, 2 * C:3 * C], g_up[:, 1, :], g_down[:, 1, :], ALU.add).then_inc(gates_ok, 1)
            dve.wait_ge(g_step, 5)
            v.tensor_tensor(rb16[:, C:2 * C], rb16[:, 0:C], bp16[:, :], ALU.mult).then_inc(gates_ok, 1)

            def ln_stats(n, b, bn):
                for t in range(NT):
                    i = v.bn_stats(stats[:, n, t, :], x_all[:, b, t * C:(t + 1) * C])
                i.then_inc(bn, 1)

            def ln_aggregate(n, mv_ok):
                for t in range(NT):
                    i = v.bn_aggr(mv[:, n, t, :], stats[:, n, t, :])
                i.then_inc(mv_ok, 1)

            def normalise(n, dst, b, ready, done):
                dve.wait_ge(ready, b + 1)
                for t in range(NT):
                    i = v.tensor_scalar(dst[:, t * C:(t + 1) * C], x_all[:, b, t * C:(t + 1) * C], mv[:, n, t, 0:1],
                                        rstd[:, n, t:t + 1], ALU.subtract, ALU.mult)
                i.then_inc(done, 1)

            def split_qk(b):
                q2 = qk[:, 0, :, :].rearrange("p t (h d) -> p (t h) d", d=HD)
                k2 = qk[:, 1, :, :].rearrange("p t (h d) -> p (t h) d", d=HD)
                if not isinstance(b, int) or b > 0:
                    dve.wait_ge(st_ps, 4 * b)
                dve.wait_ge(qk_sb, NT * (b + 1))
                for i in range(2):
                    v.tensor_scalar(stk_q[:, :, i * HD:(i + 1) * HD], q2, sig[:, 1:2], None, ALU.mult)
                    j = v.tensor_copy(stk_k[:, :, 2 * i * HD:(2 * i + 1) * HD], k2)
                j.then_inc(part_hi, 1)
                dve.wait_ge(sq_ok, b + 1)
                v.tensor_reduce(norms[:, :, :], sq[:, :, :, :].rearrange("p a t (h d) -> p (a t h) d", d=HD), AX.X, ALU.add).then_inc(norm_ok, 1)
                dve.wait_ge(part_hi, 2 * b + 1)
                v.scalar_tensor_tensor(stk_q[:, :, 2 * HD:3 * HD], q2, sig[:, 1:2], stk_q[:, :, 0:HD].bitcast(F32), ALU.mult, ALU.subtract)
                v.tensor_tensor(stk_k[:, :, HD:2 * HD], k2, stk_k[:, :, 0:HD].bitcast(F32), ALU.subtract)
                dve.wait_ge(norm_ok, b + 1)
                v.tensor_scalar(norm_rows(0), norms[:, :, :], sig[:, 2:3], None, ALU.mult).then_inc(part_hi, 1)
                dve.wait_ge(part_hi, 2 * b + 2)
                v.scalar_tensor_tensor(norm_rows(1), norms[:, :, :], sig[:, 2:3], norm_rows(0).bitcast(F32), ALU.mult, ALU.subtract).then_inc(stk_ok, 1)

            def experts(b, q, c, bank):
                dve.wait_ge(f_ps, NC * b + c + 1)
                for e in range(EC):
                    for t in range(NT):
                        j = NT * (EC * c + e) + t
                        if j < NT:
                            dve.wait_ge(acc_init, b + 1)
                        else:
                            dve.wait_ge(acc_step, NT * NE * b + j - NT + 1)
                        v.scalar_tensor_tensor(acc[:, q, t, :], work[bank][:, (t * EC + e) * C:(t * EC + e + 1) * C],
                                               mask[:, q, t, 0, EC * c + e:EC * c + e + 1], acc[:, q, t, :],
                                               ALU.mult, ALU.add).then_inc(acc_step, 1)

            def step(k, par):
                odd = (par + 1) % 2
                if has(k - 2):
                    dve.wait_ge(h2_hi_ok, k - 1)
                    v.scalar_tensor_tensor(h2_lo[:, par, :], work[2][:, 0:T], col(scale_col[:, 1, :], k - 2), h2_hi[:, par, :].bitcast(F32),
                                           ALU.mult, ALU.subtract).then_inc(h2_ok, 1)
                if has(k - 1):
                    dve.wait_ge(att_hi, k)
                    v.tensor_tensor(o_lo[:, :], att_ps[:, 0:T], o_hi[:, :].bitcast(F32), ALU.subtract).then_inc(att_ok, 1)
                if has(k + 1):
                    dve.wait_ge(t1_hi, k + 2)
                    v.scalar_tensor_tensor(h1_lo[:, :], work[0][:, 0:T], col(scale_col[:, 0, :], k + 1), h1_hi[:, :].bitcast(F32),
                                           ALU.mult, ALU.subtract).then_inc(t1_ok, 1)
                if has(k - 2):
                    b = k - 2
                    dve.wait_ge(r_ps, b + 1)
                    for t in range(NT):
                        i = v.tensor_tensor(logit[:, t, :], work[1][:, t * NE:(t + 1) * NE], rb_all[:, b, 3 * C:RB], ALU.add)
                    i.then_inc(logit_ok, 1)
                    wait_apart(dve, logit_ok, b + 1)
                    for t in range(NT):
                        i = v.max(top[:, t, :], logit[:, t, :])
                    i.then_inc(top_ok, 1)
                    wait_apart(dve, top_ok, b + 1)
                    for t in range(NT):
                        i = v.max_index(topi[:, t, :], top[:, t, :], logit[:, t, :])
                    i.then_inc(topi_ok, 1)
                    dve.wait_ge(topi_ok, b + 1)
                    v.tensor_tensor(eq[:, :, :, :], slot_e[:, :, :, :], topi[:, :, 0:2].unsqueeze(3).broadcast_to([P, NT, 2, NE]),
                                    ALU.is_equal).then_inc(eq_ok, 1)
                    dve.wait_ge(eq_ok, b + 1)
                    v.tensor_tensor(mask[:, par, :, :, :], eq[:, :, 0:1, :].broadcast_to([P, NT, 2, NE]),
                                    eq[:, :, 1:2, :].broadcast_to([P, NT, 2, NE]), ALU.add).then_inc(mask_ok, 1)
                if has(k + 1):
                    b = k + 1
                    if isinstance(k, int) and k <= 1:
                        if k == -1:
                            dve.wait_ge(ld_cb0, 16)
                            dve.wait_ge(const_ok, 6)
                    for t in range(NT):
                        bank = work[(2, 0)[t]]
                        dve.wait_ge(qkv_ps, NT * b + t + 1)
                        v.tensor_tensor(qk[:, :, t, :], bank[:, 0:2 * C].rearrange("p (a c) -> p a c", a=2),
                                        cb_all[:, b, 0:2 * C].rearrange("p (a c) -> p a c", a=2), ALU.add)
                        v.tensor_tensor(vpad[:, odd, t, :, :].rearrange("p r (g w) -> p r g w", g=G)[:, :, :, 0:HD],
                                        bank[:, 2 * C:3 * C].rearrange("p (g r d) -> p r g d", r=R, g=G),
                                        cb_all[:, b, 2 * C:3 * C].rearrange("p (g r d) -> p r g d", r=R, g=G), ALU.add).then_inc(qk_sb, 1)
                if has(k - 2):
                    experts(k - 2, par, 0, 1)
                if has(k - 1):
                    b = k - 1
                    dve.wait_ge(proj_ps, b + 1)
                    dve.wait_ge(xp_ok, b + 1)
                    v.tensor_tensor(x_all[:, b, :], work[0][:, 0:NT * C], x_all[:, b, :], ALU.add).then_inc(x1_ok, 1)
                if has(k + 1):
                    split_qk(k + 1)
                if has(k - 1):
                    wait_apart(dve, x1_ok, k)
                    ln_stats(1, k - 1, ln2_bn)
                    dve.wait_ge(ln2_bn, k)
                if has(k - 2):
                    experts(k - 2, par, 1, 1)
                if has(k - 1):
                    ln_aggregate(1, ln2_mv)
                if has(k + 2):
                    if isinstance(k, int) and k <= 0:
                        dve.wait_ge(*((ld_x0, 16), (ld_x0, 16), (rows_in, 48))[k + 2])
                    elif not isinstance(k, int):
                        dve.wait_ge(rows_in, 48 * k - 48)
                    ln_stats(0, k + 2, ln1_bn)
                    dve.wait_ge(ln1_bn, k + 3)
                if has(k - 2):
                    experts(k - 2, par, 2, 2)
                if has(k + 2):
                    ln_aggregate(0, ln1_mv)
                if has(k - 1):
                    normalise(1, x2n[:, odd, :], k - 1, ln2_rstd, x2n_ok)
                if has(k + 2):
                    normalise(0, xn[:, par, :], k + 2, ln1_rstd, xn_ok)
                if has(k - 2):
                    experts(k - 2, par, 3, 2)
                if isinstance(k, int) and k == 0:
                    dve.wait_ge(ld_fb, 32)
                    v.tensor_copy(fb_h[:, :, :], fb_f32[:, :, :]).then_inc(fb_h_ok, 1)
                    dve.wait_ge(fb_h_ok, 1)
                    v.scalar_tensor_tensor(fb_all[:, :, :], fb_h[:, :, :].bitcast(F32), lo_rows[:, 0:1], fb_f32[:, :, :],
                                           ALU.mult, ALU.add).then_inc(fb_ok, 1)
                if isinstance(k, int) and k == -1:
                    dve.wait_ge(we_hi_ok, 1)
                    v.tensor_tensor(we_lo[:, :], we_t[:, :], we_hi[:, :].bitcast(F32), ALU.subtract).then_inc(we_ok, 1)
                    dve.wait_ge(fb_ps, 1)
                    dve.wait_ge(ld_be, 16)
                    dve.wait_ge(ld_br, 16)
                    for n, w in enumerate((512, 512, NE)):
                        i = v.tensor_tensor(fb16[:, 512 * n:512 * n + w], scores[0:NB, n, 0:w], be16[:, 512 * n:512 * n + w], ALU.add)
                    i.then_inc(fb_sb, 1)
                    dve.wait_ge(fb_sb, 1)
                    dve.wait_ge(gates_ok, 2)
                    v.tensor_copy(rb16[:, 3 * C:RB], fb16[:, NE * C:NW]).then_inc(rb_ok, 1)

            steps(dve, step)

        @block.tensor
        def _(pe):
            pe.wait_ge(ident_ok, 1)
            pe.wait_ge(c_silu, 1)
            pe.transpose(work[0][:, 0:NB], c_sb[:, 1, :], ident[0:NB, 0:NB]).then_inc(ct_ps, 1)
            pe.wait_ge(ct_sb, 1)
            pe.wait_ge(ld_mod, 16)
            for j, m in enumerate((0, 1, 3, 4)):
                i = pe.matmul(work[1][:, j * NB:(j + 1) * NB], w_mod_sb[:, m * C:(m + 1) * C], s_t[:, :], start=True, stop=True)
            i.then_inc(mod_ps, 1)
            for j, m in enumerate((2, 5)):
                i = pe.matmul(scores[0:NB, 3, j * C:(j + 1) * C], s_t[:, :], w_mod_sb[:, m * C:(m + 1) * C], start=True, stop=True)
            i.then_inc(gate_ps, 1)
            pe.wait_ge(mod_sb, 2)
            pe.wait_ge(ld_qkv, 16)
            pe.matmul(work[2][0:NB, 0:NQKV], shift_col[:, 0, :], wqkv_sb[:, :], start=True, stop=True).then_inc(cb_ps, 1)

            def three(dst, a_hi, a_lo, b_hi, b_lo):
                pe.matmul(dst, a_hi, b_hi, start=True, stop=False)
                pe.matmul(dst, a_lo, b_hi, start=False, stop=False)
                return pe.matmul(dst, a_hi, b_lo, start=False, stop=True)

            def expert_weights():
                pe.wait_ge(ld_we, 16)
                pe.wait_ge(ld_wr, 16)
                for e in range(NE):
                    pe.transpose(scores[:, e // 4, (e % 4) * C:(e % 4 + 1) * C], we_sb[:, e, :], ident[:, :])
                pe.transpose(scores[:, 2, 0:NE], wr_sb[:, :], ident[0:NE, 0:NE]).then_inc(wet_ps, 1)
                pe.wait_ge(wet_sb, 1)
                for n, w in enumerate((512, 512, NE)):
                    i = pe.matmul(scores[0:NB, n, 0:w], shift_col[:, 1, :], we_t[:, 512 * n:512 * n + w], start=True, stop=True)
                i.then_inc(fb_ps, 1)

            def warm_up(n):
                for _ in range(n):
                    pe.matmul(att_ps[:, 0:NQKV], wq_hi[:, 0:P], wq_hi[:, :], start=True, stop=True)

            def qk_scores(k, par, g):
                n = 4 * k + g
                pe.wait_ge(st_sb, 4 * k + g + 1)
                if isinstance(k, int) and k == 0 and g == 0:
                    pe.wait_ge(fb_sb, 1)
                for half in range(2):
                    if not isinstance(n, int) or n > 0:
                        pe.wait_ge((exp_a, exp_b)[half], n)
                    for t in range(NT):
                        for r in (2 * half, 2 * half + 1):
                            rows = slice(r * ROWS, (r + 1) * ROWS)
                            i = pe.matmul(scores[:, r, t * T:(t + 1) * T], st_t[rows, par, g, t * P:(t + 1) * P],
                                          st_t[rows, par, g, T:2 * T], start=True, stop=True)
                    i.then_inc((qk_a, qk_b)[half], 1)

            def pv(b, q, g):
                pe.wait_ge(exp_a, 4 * b + g + 1)
                pe.wait_ge(exp_b, 4 * b + g + 1)
                if g == 0:
                    pe.wait_ge(qk_sb, NT * (b + 1))
                    if not isinstance(b, int) or b > 0:
                        pe.wait_ge(att_ok, b)
                for t in range(NT):
                    for r in range(R):
                        i = pe.matmul(att_ps[r * ROWS:(r + 1) * ROWS, 0:T], vpad[:, q, t, r, g * ROWS:(g + 1) * ROWS],
                                      probs[:, g, r, t * T:(t + 1) * T], start=(g == 0 and t == 0), stop=(g == G - 1 and t == NT - 1))
                i.then_inc(pv_done, 1)

            def stack(b, g, bank):
                for a, src in enumerate((stk_q, stk_k)):
                    for t in range(NT):
                        heads = src[:, t * H + g * R:t * H + (g + 1) * R, :].bitcast(F32).rearrange("p r w -> p (r w)")
                        i = pe.transpose(work[bank][:, a * T + t * P:a * T + (t + 1) * P], heads, ident[:, :])
                i.then_inc(st_ps, 1)

            def expert_chunk(b, q, c, bank):
                for t in range(NT):
                    ts = slice(t * P, (t + 1) * P)
                    ws = slice(c * EC * C, (c + 1) * EC * C)
                    i = three(work[bank][:, t * EC * C:(t + 1) * EC * C], h2_hi[:, q, ts], h2_lo[:, q, ts], we_hi[:, ws], we_lo[:, ws])
                i.then_inc(f_ps, 1)

            def step(k, par):
                odd = (par + 1) % 2
                if has(k):
                    qk_scores(k, par, 0)
                    pe.wait_ge(st_sb, 4 * k + 1)
                    stack(k, 2, 0)
                    pe.wait_ge(st_sb, 4 * k + 2)
                    stack(k, 3, 1)
                if has(k - 2):
                    pe.wait_ge(x2n_ok, k - 1)
                    if not isinstance(k, int) or k > 2:
                        pe.wait_ge(acc_step, NT * NE * (k - 2))
                    for t in range(NT):
                        i = pe.transpose(work[2][:, t * P:(t + 1) * P], x2n[:, par, t * C:(t + 1) * C], ident[:, :])
                    i.then_inc(h2_ps, 1)
                if has(k - 1):
                    pv(k - 1, odd, 3)
                if has(k + 1):
                    pe.wait_ge(xn_ok, k + 2)
                    if has(k):
                        pe.wait_ge(st_sb, 4 * k + 3)
                    for t in range(NT):
                        i = pe.transpose(work[0][:, t * P:(t + 1) * P], xn[:, odd, t * C:(t + 1) * C], ident[:, :])
                    i.then_inc(t1_ps, 1)
                if has(k):
                    qk_scores(k, par, 1)
                if has(k - 2):
                    pe.wait_ge(h2_ok, k - 1)
                    if isinstance(k, int) and k == 2:
                        pe.wait_ge(we_ok, 1)
                    for t in range(NT):
                        i = three(work[1][:, t * NE:(t + 1) * NE], h2_hi[:, par, t * P:(t + 1) * P], h2_lo[:, par, t * P:(t + 1) * P],
                                  we_hi[:, NE * C:NW], we_lo[:, NE * C:NW])
                    i.then_inc(r_ps, 1)
                if has(k):
                    pv(k, par, 0)
                if has(k + 1):
                    pe.wait_ge(t1_ok, k + 2)
                    if isinstance(k, int) and k == -1:
                        pe.wait_ge(wq_ok, 1)
                        pe.wait_ge(cb_sb, 1)
                    for t in range(NT):
                        i = three(work[(2, 0)[t]][:, 0:NQKV], h1_hi[:, t * P:(t + 1) * P], h1_lo[:, t * P:(t + 1) * P], wq_hi[:, :], wq_lo[:, :])
                        i.then_inc(qkv_ps, 1)
                if has(k - 2):
                    pe.wait_ge(mask_ok, k - 1)
                    for t in range(NT):
                        i = pe.transpose(work[1][0:2 * NE, T + t * P:T + (t + 1) * P], mask[:, par, t, :, :].rearrange("p a e -> p (a e)"), ident[:, :])
                    i.then_inc(m_ps, 1)
                if has(k):
                    qk_scores(k, par, 2)
                if has(k - 2):
                    pe.wait_ge(m_sb, k - 1)
                    expert_chunk(k - 2, par, 0, 1)
                    pe.wait_ge(fbb_ok, k - 1)
                    if has(k + 1):
                        pe.wait_ge(qk_sb, NT * (k + 1) + 1)
                    for t in range(NT):
                        i = pe.matmul(work[2][:, t * C:(t + 1) * C], mask_t[:, t * P:(t + 1) * P], fb_b[:, :], start=True, stop=True)
                    i.then_inc(b_ps, 1)
                if has(k):
                    pv(k, par, 1)
                if has(k - 1):
                    pe.wait_ge(att_ok, k)
                    pe.wait_ge(wg_ok, k)
                    if has(k + 1):
                        pe.wait_ge(qk_sb, NT * (k + 2))
                    for t in range(NT):
                        i = three(work[0][:, t * C:(t + 1) * C], o_hi[:, t * P:(t + 1) * P], o_lo[:, t * P:(t + 1) * P],
                                  wg_hi[:, odd, :], wg_lo[:, odd, :])
                    i.then_inc(proj_ps, 1)
                if has(k - 2):
                    pe.wait_ge(acc_step, NT * NE * (k - 2) + NT * EC)
                    expert_chunk(k - 2, par, 1, 1)
                if has(k):
                    qk_scores(k, par, 3)
                if has(k - 2):
                    pe.wait_ge(acc_init, k - 1)
                    expert_chunk(k - 2, par, 2, 2)
                if has(k):
                    pv(k, par, 2)
                if isinstance(k, int) and k == -1:
                    expert_weights()
                    warm_up(WARM)
                if has(k + 1):
                    pe.wait_ge(stk_ok, k + 2)
                    if has(k - 1):
                        pe.wait_ge(x1_ok, k)
                    stack(k + 1, 0, 0)
                    if has(k - 2):
                        pe.wait_ge(acc_step, NT * NE * (k - 2) + 2 * NT * EC)
                    stack(k + 1, 1, 1)
                if has(k - 2):
                    pe.wait_ge(acc_step, NT * NE * (k - 2) + 3 * NT * EC)
                    expert_chunk(k - 2, par, 3, 2)

            steps(pe, step)


_INS = ['L0_attn_x', 'L0_attn_Wqkv', 'L0_attn_bqkv', 'L0_attn_r_sigma', 'L0_attn_Wproj', 'L0_attn_bproj',
        'L0_ffn_w_router', 'L0_ffn_b_router', 'L0_ffn_w_experts', 'L0_ffn_b_experts', 'L0_c', 'L0_wmod']


def kernel(**inputs):
    import numpy as _np
    import concourse.bacc as _bacc
    from concourse import mybir as _mybir
    from concourse.bass_utils import run_bass_kernel_spmd as _run

    nc = _bacc.Bacc("TRN2", target_bir_lowering=False, num_devices=1)
    arrays, args = {}, []
    for name in _INS:
        a = _np.ascontiguousarray(inputs[name])
        if name == 'L0_attn_r_sigma':
            a = a.reshape(1)
        arrays[f"in_{name}_dram"] = a
        args.append(nc.dram_tensor(f"in_{name}_dram", a.shape, _mybir.dt.from_np(a.dtype), kind="ExternalInput").ap())
    shape = inputs['L0_attn_x'].shape
    args.append(nc.dram_tensor("out_dram", shape, _mybir.dt.float32, kind="ExternalOutput").ap())
    adaln_block(nc, *args)
    r = _run(nc, [arrays], core_ids=[0])
    return r.results[0]["out_dram"]
```

```python
from contextlib import ExitStack

import concourse.bass as bass
from concourse import mybir

F32 = mybir.dt.float32
F32R = mybir.dt.float32r
U32 = mybir.dt.uint32
ALU = mybir.AluOpType
ACT = mybir.ActivationFunctionType
AX = mybir.AxisListType

LN_EPS = 1e-5
GATE_MIN = 0.25
WARM = 20
LOOK = 5


def adaln_block(nc, x, w_qkv, b_qkv, sigma, w_proj, b_proj, w_router, b_router, w_experts, b_experts, cond, w_mod, out):
    NB, T, C = x.shape
    P = 128
    NT = T // P
    NE = w_router.shape[0]
    HD = 8
    H = C // HD
    R = 4
    G = H // R
    ROWS = P // R
    VBLK = 160
    NC = 4
    EC = NE // NC
    RB = 3 * C + NE
    U = 4
    STEPS = NE * NT
    NP = 4
    NQKV = 3 * C
    NW = NE * C + NE

    xv = x.rearrange("b (p t) c -> b p (t c)", t=NT)
    ov = out.rearrange("b (p t) c -> b p (t c)", t=NT)

    cb_dram = nc.dram_tensor("cb_rows", [NB, NQKV], F32).ap()
    rb_dram = nc.dram_tensor("rb_rows", [NB, RB], F32).ap()
    fb_dram = nc.dram_tensor("fb_rows", [NB, NE * C], F32).ap()

    with ExitStack() as ctx:
        def sb(name, shape, dt=F32):
            return ctx.enter_context(nc.sbuf_tensor(name, shape, dt))

        def sem(name):
            return ctx.enter_context(nc.semaphore(name))

        scores = ctx.enter_context(nc.psum_tensor("scores", [P, R, NT * T], F32))
        att_ps = ctx.enter_context(nc.psum_tensor("att_ps", [P, 512], F32))
        work = [ctx.enter_context(nc.psum_tensor(f"work{i}", [P, 512], F32)) for i in range(3)]

        x_all = sb("x_all", [P, NB, NT * C])
        cb_all = sb("cb_all", [P, NB, NQKV])
        rb_all = sb("rb_all", [P, NB, RB])
        fb_all = sb("fb_all", [2 * NE, NB, C], F32R)
        ident = sb("ident", [P, P])
        ident_r = sb("ident_r", [P, P], F32R)
        wq_hi = sb("wq_hi", [P, NQKV], F32R)
        wq_lo = sb("wq_lo", [P, NQKV], F32R)
        we_hi = sb("we_hi", [P, NE * C], F32R)
        we_lo = sb("we_lo", [P, NE * C], F32R)
        wr_parts = sb("wr_parts", [P, 2 * NE], F32R)
        wproj_sb = sb("wproj_sb", [P, C])
        scale_col = sb("scale_col", [P, 2, NB])
        sig = sb("sig", [P, 3])
        expo = sb("expo", [P, NT])
        eps = sb("eps", [P, NT])
        slot_e = sb("slot_e", [P, NT, 2, NE])

        stats = sb("stats", [P, 2, NT, 6])
        mv = sb("mv", [P, 2, NT, 2])
        ve = sb("ve", [P, 2, NT])
        rstd = sb("rstd", [P, 2, NT])
        xn = sb("xn", [P, 2, NT * C])
        h1_hi = sb("h1_hi", [P, T], F32R)
        h1_lo = sb("h1_lo", [P, T], F32R)
        qk = sb("qk", [P, 2, NT, C])
        sq = sb("sq", [P, 2, NT, C])
        norms = sb("norms", [P, 2, NT * H])
        stk = sb("stk", [P, 2 * (NT * H * ROWS + 2)], F32R)
        st_t = sb("st_t", [P, 2, G, 2 * T], F32R)
        vpad = sb("vpad", [P, 2, NT, R, VBLK])
        probs = sb("probs", [P, NP, R, NT * T])
        o_hi = sb("o_hi", [P, T], F32R)
        o_lo = sb("o_lo", [P, T], F32R)
        wg = sb("wg", [P, C])
        wg_hi = sb("wg_hi", [P, 2, C], F32R)
        wg_lo = sb("wg_lo", [P, 2, C], F32R)
        x2n = sb("x2n", [P, 2, NT * C])
        h2_hi = sb("h2_hi", [P, 2, T], F32R)
        h2_lo = sb("h2_lo", [P, 2, T], F32R)
        logit = sb("logit", [P, NT, NE])
        top = sb("top", [P, NT, NE])
        topi = sb("topi", [P, NT, NE], U32)
        eq = sb("eq", [P, NT, 2, NE])
        mask = sb("mask", [P, 2, NT, 2, NE])
        mask_t = sb("mask_t", [2 * NE, T], F32R)
        fb_b = sb("fb_b", [2 * NE, C], F32R)
        acc = sb("acc", [P, 2, NT, C])
        gated = sb("gated", [P, NT * C])

        spare = probs[:, :, :, :].rearrange("p a r n -> p (a r n)")
        w_mod_sb = spare[:, 0:6 * C]
        wqkv_sb = sb("wqkv_sb", [P, NQKV])
        wr_sb = sb("wr_sb", [NE, C])
        we_sb = spare[:, 1024:1024 + NE * C].rearrange("p (e c) -> p e c", e=NE)
        we_t = spare[:, 2048:2048 + NW]
        c_sb = sb("c_sb", [NB, 3, C])
        s_t = sb("s_t", [P, NB])
        shift_col = sb("shift_col", [P, 2, NB])
        bq16 = sb("bq16", [NB, NQKV])
        bp16 = sb("bp16", [NB, C])
        be16 = spare[0:NB, 4096:4096 + NW]
        cb16 = sb("cb16", [NB, NQKV])
        rb16 = sb("rb16", [NB, RB])
        fb16 = sb("fb16", [NB, NW])
        g_up = sb("g_up", [NB, 2, C])
        g_down = sb("g_down", [NB, 2, C])
        fb_f32 = sb("fb_f32", [2 * NE, NB, C])
        fb_h = sb("fb_h", [2 * NE, NB, C], F32R)
        lo_rows = sb("lo_rows", [2 * NE, 1])

        ld_c = sem("ld_c")
        ld_mod = sem("ld_mod")
        ld_qkv = sem("ld_qkv")
        ld_x0 = sem("ld_x0")
        ld_bq = sem("ld_bq")
        ld_bp = sem("ld_bp")
        ld_sig = sem("ld_sig")
        rows_in = sem("rows_in")
        ld_we = sem("ld_we")
        ld_wr = sem("ld_wr")
        ld_be = sem("ld_be")
        ld_br = sem("ld_br")
        ld_proj = sem("ld_proj")
        st_cb = sem("st_cb")
        st_rb = sem("st_rb")
        st_fb = sem("st_fb")
        ld_cb0 = sem("ld_cb0")
        ld_fb = sem("ld_fb")
        stored = sem("stored")
        ident_z = sem("ident_z")
        ident_ok = sem("ident_ok")
        ident_r_ok = sem("ident_r_ok")
        const_ok = sem("const_ok")
        expo_ok = sem("expo_ok")
        c_exp = sem("c_exp")
        c_den = sem("c_den")
        c_rec = sem("c_rec")
        c_silu = sem("c_silu")
        ct_ps = sem("ct_ps")
        ct_sb = sem("ct_sb")
        mod_ps = sem("mod_ps")
        gate_ps = sem("gate_ps")
        mod_sb = sem("mod_sb")
        cb_ps = sem("cb_ps")
        cb_sb = sem("cb_sb")
        sig_ok = sem("sig_ok")
        g_step = sem("g_step")
        gates_ok = sem("gates_ok")
        wq_hi_ok = sem("wq_hi_ok")
        wq_ok = sem("wq_ok")
        wet_ps = sem("wet_ps")
        wet_sb = sem("wet_sb")
        we_hi_ok = sem("we_hi_ok")
        we_ok = sem("we_ok")
        fb_ps = sem("fb_ps")
        fb_sb = sem("fb_sb")
        rb_ok = sem("rb_ok")
        fb_h_ok = sem("fb_h_ok")
        fb_ok = sem("fb_ok")
        ln1_bn = sem("ln1_bn")
        ln1_mv = sem("ln1_mv")
        ln1_ve = sem("ln1_ve")
        ln1_rstd = sem("ln1_rstd")
        xn_ok = sem("xn_ok")
        t1_ps = sem("t1_ps")
        t1_hi = sem("t1_hi")
        t1_ok = sem("t1_ok")
        qkv_ps = sem("qkv_ps")
        qk_sb = sem("qk_sb")
        sq_ok = sem("sq_ok")
        norm_ok = sem("norm_ok")
        part_k = sem("part_k")
        part_q = sem("part_q")
        norm_hi = sem("norm_hi")
        stk_ok = sem("stk_ok")
        st_ps = sem("st_ps")
        st_sb = sem("st_sb")
        qk_a = sem("qk_a")
        qk_b = sem("qk_b")
        exp_a = sem("exp_a")
        exp_b = sem("exp_b")
        pv_done = sem("pv_done")
        att_hi = sem("att_hi")
        att_ok = sem("att_ok")
        wg_h = sem("wg_h")
        wg_ok = sem("wg_ok")
        xp_ok = sem("xp_ok")
        proj_ps = sem("proj_ps")
        x1_ok = sem("x1_ok")
        ln2_bn = sem("ln2_bn")
        ln2_mv = sem("ln2_mv")
        ln2_ve = sem("ln2_ve")
        ln2_rstd = sem("ln2_rstd")
        x2n_ok = sem("x2n_ok")
        h2_ps = sem("h2_ps")
        h2_hi_ok = sem("h2_hi_ok")
        h2_ok = sem("h2_ok")
        r_ps = sem("r_ps")
        lsum_ok = sem("lsum_ok")
        logit_ok = sem("logit_ok")
        top_ok = sem("top_ok")
        topi_ok = sem("topi_ok")
        eq_ok = sem("eq_ok")
        mask_ok = sem("mask_ok")
        m_ps = sem("m_ps")
        m_sb = sem("m_sb")
        fbb_ok = sem("fbb_ok")
        b_ps = sem("b_ps")
        acc_init = sem("acc_init")
        f_ps = sem("f_ps")
        acc_step = sem("acc_step")
        gated_ok = sem("gated_ok")
        res_ok = sem("res_ok")

        stk_q = stk[:, 0:NT * H * ROWS].rearrange("p (h w) -> p h w", w=ROWS)
        stk_k = stk[:, NT * H * ROWS:2 * NT * H * ROWS].rearrange("p (h w) -> p h w", w=ROWS)
        stk_qk = stk[:, :].rearrange("p (a n) -> p a n", a=2)
        NQ = 3 * HD

        def norm_rows(i):
            return stk_qk[:, :, NQ + i:NQ + i + (NT * H - 1) * ROWS + 1:ROWS]

        hi_rows_q = stk_q[:, :, 0:2 * HD].rearrange("p h (i d) -> p h i d", i=2)
        hi_rows_k = stk_k[:, :, :].rearrange("p h (i d) -> p h i d", i=2)[:, :, :, 0:HD]

        def twice(a):
            return qk[:, a, :, :].rearrange("p t (h d) -> p (t h) d", d=HD).unsqueeze(2).broadcast_to([P, NT * H, 2, HD])

        block = ctx.enter_context(nc.Block())

        def has(b):
            return not isinstance(b, int) or 0 <= b < NB

        def steps(eng, step):
            for k in range(-2, U):
                step(k, k % 2)
            with eng.Fori(1, NB // U - 1, 1) as i:
                for u in range(U):
                    step(U * i + u, u % 2)
            for k in range(NB - U, NB + 3):
                step(k, k % 2)

        def wait_apart(eng, semaphore, value):
            eng.wait_ge(ident_ok, 1)
            eng.wait_ge(semaphore, value)

        def col(t, b):
            return t[:, bass.ds(b, 1)]

        @block.sync
        def _(sp):
            sp.dma_start(c_sb[:, 0, :], cond).then_inc(ld_c, 16)
            sp.dma_start(w_mod_sb[:, :], w_mod).then_inc(ld_mod, 16)
            sp.dma_start(x_all[:, 0:2, :], xv[0:2].rearrange("b p n -> p b n")).then_inc(ld_x0, 16)
            sp.dma_start(sig[:, 0:1], sigma.partition_broadcast(P)).then_inc(ld_sig, 16)
            sp.dma_start(we_sb[:, :, :], w_experts.rearrange("e o d -> o e d")).then_inc(ld_we, 16)
            sp.dma_start(wr_sb[:, :], w_router).then_inc(ld_wr, 16)
            sp.dma_start(be16[:, 0:NE * C], b_experts.rearrange("e o -> (e o)").partition_broadcast(NB)).then_inc(ld_be, 16)
            sp.dma_start(be16[:, NE * C:NW], b_router.partition_broadcast(NB)).then_inc(ld_br, 16)
            sp.wait_ge(cb_sb, 1)
            sp.dma_start(cb_dram, cb16[:, :]).then_inc(st_cb, 16)
            sp.wait_ge(st_cb, 16)
            sp.dma_start(cb_all[:, 0:2, :], cb_dram[0:2].partition_broadcast(P)).then_inc(ld_cb0, 16)
            sp.wait_ge(fb_sb, 1)
            sp.dma_start(fb_dram, fb16[:, 0:NE * C]).then_inc(st_fb, 16)
            sp.wait_ge(rb_ok, 1)
            sp.dma_start(rb_dram, rb16[:, :]).then_inc(st_rb, 16)
            sp.wait_ge(st_fb, 16)
            for half in range(2):
                sp.dma_start(fb_f32[half * NE:(half + 1) * NE, :, :],
                             fb_dram.rearrange("b (e o) -> e b o", e=NE)).then_inc(ld_fb, 16)
            sp.wait_ge(st_rb, 16)
            sp.dma_start(rb_all[:, 0:LOOK, :], rb_dram[0:LOOK].partition_broadcast(P)).then_inc(rows_in, 16)
            sp.dma_start(cb_all[:, 2:LOOK, :], cb_dram[2:LOOK].partition_broadcast(P)).then_inc(rows_in, 16)

            def store(b):
                sp.wait_ge(res_ok, b + 1)
                sp.dma_start(ov[b], x_all[:, b, :]).then_inc(stored, 16)

            with sp.Fori(0, NB - LOOK, 1) as b:
                sp.wait_ge(rows_in, 48 * b + 48)
                n = b + LOOK
                sp.dma_start(x_all[:, n, :], xv[n]).then_inc(rows_in, 16)
                sp.dma_start(cb_all[:, n, :], cb_dram[n].partition_broadcast(P)).then_inc(rows_in, 16)
                sp.dma_start(rb_all[:, n, :], rb_dram[n].partition_broadcast(P)).then_inc(rows_in, 16)
                store(b)
            with sp.Fori(NB - LOOK, NB, 1) as b:
                store(b)
            sp.wait_ge(stored, 16 * NB)

        @block.gpsimd
        def _(pool):
            nc.gpsimd.memset(ident[:, :], 0.0).then_inc(ident_z, 1)
            nc.gpsimd.memset(lo_rows[:, :], 0.0).then_inc(ident_z, 1)
            pool.wait_ge(ident_z, 2)
            nc.gpsimd.affine_select(out=ident[:, :], in_=ident[:, :], compare_op=ALU.not_equal, fill=1.0, base=0,
                                    pattern=[[-1, P]], channel_multiplier=1).then_inc(ident_ok, 1)
            nc.gpsimd.affine_select(out=lo_rows[:, :], in_=lo_rows[:, :], compare_op=ALU.is_ge, fill=-1.0, base=NE - 1,
                                    pattern=[[0, 1]], channel_multiplier=-1).then_inc(const_ok, 1)
            nc.gpsimd.memset(expo[:, :], -0.5).then_inc(expo_ok, 1)
            nc.gpsimd.memset(eps[:, :], LN_EPS).then_inc(expo_ok, 1)
            nc.gpsimd.memset(stk[:, :].bitcast(F32), 0.0).then_inc(const_ok, 1)
            nc.gpsimd.memset(vpad[:, :, :, :, :].rearrange("p a t r n -> p (a t r n)"), 0.0).then_inc(const_ok, 1)
            nc.gpsimd.iota(slot_e[:, :, :, :], [[0, NT], [0, 2], [1, NE]], base=0, channel_multiplier=0,
                           allow_small_or_imprecise_dtypes=True).then_inc(const_ok, 1)
            pool.wait_ge(const_ok, 4)
            nc.gpsimd.memset(stk_q[:, :, NQ + 2:NQ + 4].bitcast(F32), 1.0).then_inc(const_ok, 1)
            nc.gpsimd.memset(stk_k[:, :, NQ:NQ + 2].bitcast(F32), 1.0).then_inc(const_ok, 1)

            def rsqrt(n, b, bn, ve_ok, done):
                wait_apart(pool, bn, b + 1)
                nc.gpsimd.tensor_tensor(ve[:, n, :], mv[:, n, :, 1], eps[:, :], ALU.add).then_inc(ve_ok, 1)
                wait_apart(pool, ve_ok, b + 1)
                nc.gpsimd.tensor_tensor(rstd[:, n, :], ve[:, n, :], expo[:, :], ALU.pow).then_inc(done, 1)

            def step(k, par):
                odd = (par + 1) % 2
                if has(k + 2):
                    rsqrt(0, k + 2, ln1_mv, ln1_ve, ln1_rstd)
                if has(k - 2):
                    b = k - 2
                    if has(k - 3):
                        wait_apart(pool, b_ps, b)
                    else:
                        pool.wait_ge(fb_ok, 1)
                    nc.gpsimd.tensor_copy(fb_b[:, :], fb_all[:, b, :].bitcast(F32)).then_inc(fbb_ok, 1)
                if has(k - 1):
                    b = k - 1
                    if has(k - 2):
                        wait_apart(pool, wg_ok, b)
                    else:
                        pool.wait_ge(rows_in, 48)
                        pool.wait_ge(ld_proj, 16 * R)
                    nc.gpsimd.tensor_tensor(wg[:, :], wproj_sb[:, :], rb_all[:, b, 0:C], ALU.mult)
                    nc.gpsimd.tensor_tensor(wg_hi[:, odd, :], wproj_sb[:, :], rb_all[:, b, 0:C], ALU.mult).then_inc(wg_h, 1)
                    wait_apart(pool, wg_h, b + 1)
                    nc.gpsimd.tensor_tensor(wg_lo[:, odd, :], wg[:, :], wg_hi[:, odd, :].bitcast(F32), ALU.subtract).then_inc(wg_ok, 1)
                    for t in range(NT):
                        xs = x_all[:, b, t * C:(t + 1) * C]
                        i = nc.gpsimd.tensor_tensor(xs, xs, rb_all[:, b, C:2 * C], ALU.add)
                    i.then_inc(xp_ok, 1)
                if has(k + 1):
                    b = k + 1
                    for t in range(NT):
                        pool.wait_ge(qk_sb, NT * b + t + 1)
                        i = nc.gpsimd.tensor_tensor(sq[:, :, t, :], qk[:, :, t, :], qk[:, :, t, :], ALU.mult)
                    i.then_inc(sq_ok, 1)
                if has(k - 3):
                    b = k - 3
                    wait_apart(pool, acc_step, STEPS * (b + 1))
                    if not has(k - 1):
                        pool.wait_ge(res_ok, b)
                    for t in range(NT):
                        i = nc.gpsimd.tensor_tensor(gated[:, t * C:(t + 1) * C], acc[:, odd, t, :], rb_all[:, b, 2 * C:3 * C], ALU.mult)
                    i.then_inc(gated_ok, 1)
                    wait_apart(pool, gated_ok, b + 1)
                    nc.gpsimd.tensor_tensor(x_all[:, b, :], x_all[:, b, :], gated[:, :], ALU.add).then_inc(res_ok, 1)
                if has(k - 1):
                    rsqrt(1, k - 1, ln2_mv, ln2_ve, ln2_rstd)

            steps(pool, step)

        @block.scalar
        def _(act):
            act.dma_start(wqkv_sb[:, :], w_qkv).then_inc(ld_qkv, 16)
            act.dma_start(bq16[:, :], b_qkv.partition_broadcast(NB)).then_inc(ld_bq, 16)
            act.dma_start(bp16[:, :], b_proj.partition_broadcast(NB)).then_inc(ld_bp, 16)
            for r in range(R):
                act.dma_start(wproj_sb[r * ROWS:(r + 1) * ROWS, :],
                              w_proj.rearrange("(g r d) n -> r g d n", g=G, r=R)[r]).then_inc(ld_proj, 16)
            act.dma_start(x_all[:, 2:LOOK, :], xv[2:LOOK].rearrange("b p n -> p b n")).then_inc(rows_in, 16)
            act.wait_ge(ld_c, 16)
            nc.scalar.activation(c_sb[:, 1, :], c_sb[:, 0, :], ACT.Exp, scale=-1.0).then_inc(c_exp, 1)
            act.wait_ge(ld_qkv, 16)
            nc.scalar.copy(wq_hi[:, :], wqkv_sb[:, :]).then_inc(wq_hi_ok, 1)

            def expert_weights():
                act.wait_ge(wet_ps, 1)
                nc.scalar.copy(we_t[:, 0:2 * 512], scores[:, 0:2, :].rearrange("p r n -> p (r n)"))
                nc.scalar.copy(we_t[:, NE * C:NW], scores[:, 2, 0:NE]).then_inc(wet_sb, 1)
                act.wait_ge(wet_sb, 1)
                nc.scalar.copy(we_hi[:, :], we_t[:, 0:NE * C])
                nc.scalar.copy(wr_parts[:, 0:NE], we_t[:, NE * C:NW]).then_inc(we_hi_ok, 1)

            def exp(k, g, half):
                n = 4 * k + g
                done = (exp_a, exp_b)[half]
                act.wait_ge((qk_a, qk_b)[half], n + 1)
                if not isinstance(n, int) or n >= NP:
                    act.wait_ge(pv_done, n - NP + 1)
                nc.scalar.activation(probs[:, g, 2 * half:2 * half + 2, :], scores[:, 2 * half:2 * half + 2, :], ACT.Exp).then_inc(done, 1)

            def stack_out(b, q, g, bank):
                act.wait_ge(st_ps, 4 * b + g + 1)
                nc.scalar.copy(st_t[:, q, g, :], work[bank][:, :]).then_inc(st_sb, 1)

            def step(k, par):
                odd = (par + 1) % 2
                a, b, c = range(3)
                if has(k):
                    exp(k, 0, 0)
                    stack_out(k, par, 2, b)
                    stack_out(k, par, 3, c)
                    exp(k, 0, 1)
                if has(k - 1):
                    act.wait_ge(pv_done, 4 * k)
                    nc.scalar.copy(o_hi[:, :], att_ps[:, 0:T]).then_inc(att_hi, 1)
                if has(k - 2):
                    act.wait_ge(h2_ps, k - 1)
                    nc.scalar.activation(h2_hi[:, par, :], work[b][:, 0:T], ACT.Identity, scale=col(scale_col[:, 1, :], k - 2)).then_inc(h2_hi_ok, 1)
                if has(k + 1):
                    act.wait_ge(t1_ps, k + 2)
                    nc.scalar.activation(h1_hi[:, :], work[c][:, 0:T], ACT.Identity, scale=col(scale_col[:, 0, :], k + 1)).then_inc(t1_hi, 1)
                if has(k):
                    exp(k, 1, 0)
                    exp(k, 1, 1)
                if has(k):
                    exp(k, 2, 0)
                if has(k):
                    exp(k, 2, 1)
                if has(k - 2):
                    act.wait_ge(m_ps, k - 1)
                    nc.scalar.copy(mask_t[:, :], work[a][0:2 * NE, T:2 * T]).then_inc(m_sb, 1)
                if has(k + 1):
                    n = k + 1
                    if has(k):
                        act.wait_ge(st_ps, 4 * n)
                    elif isinstance(k, int) and k == -1:
                        act.wait_ge(sig_ok, 2)
                        act.wait_ge(const_ok, 6)
                    act.wait_ge(qk_sb, NT * (n + 1))
                    nc.scalar.copy(hi_rows_k, twice(1)).then_inc(part_k, 1)
                if has(k + 1):
                    nc.scalar.activation(hi_rows_q, twice(0), ACT.Identity, scale=sig[:, 1:2]).then_inc(part_q, 1)
                if has(k - 2):
                    act.wait_ge(b_ps, k - 1)
                    nc.scalar.copy(acc[:, par, :, :].rearrange("p t c -> p (t c)"), work[a][:, 0:NT * C]).then_inc(acc_init, 1)
                if has(k):
                    exp(k, 3, 0)
                    exp(k, 3, 1)
                if isinstance(k, int) and k == -1:
                    expert_weights()
                if has(k + 1):
                    stack_out(k + 1, odd, 0, c)
                    stack_out(k + 1, odd, 1, a)

            steps(act, step)

        @block.vector
        def _(dve):
            v = nc.vector
            dve.wait_ge(c_exp, 1)
            v.tensor_scalar(c_sb[:, 1, :], c_sb[:, 1, :], 1.0, None, ALU.add).then_inc(c_den, 1)
            dve.wait_ge(c_den, 1)
            v.reciprocal(c_sb[:, 2, :], c_sb[:, 1, :]).then_inc(c_rec, 1)
            dve.wait_ge(c_rec, 1)
            v.tensor_tensor(c_sb[:, 1, :], c_sb[:, 0, :], c_sb[:, 2, :], ALU.mult).then_inc(c_silu, 1)
            dve.wait_ge(ct_ps, 1)
            v.tensor_copy(s_t[:, :], work[0][:, 0:NB]).then_inc(ct_sb, 1)
            v.tensor_copy(ident_r[:, :], ident[:, :]).then_inc(ident_r_ok, 1)
            dve.wait_ge(mod_ps, 1)
            mod_cols = work[1][:, 0:4 * NB].rearrange("p (m b) -> p m b", m=4)
            v.tensor_copy(shift_col[:, :, :], mod_cols[:, 0:4:2, :]).then_inc(mod_sb, 1)
            v.tensor_scalar(scale_col[:, :, :], mod_cols[:, 1:4:2, :], 1.0, None, ALU.add).then_inc(mod_sb, 1)
            dve.wait_ge(wq_hi_ok, 1)
            v.tensor_tensor(wq_lo[:, :], wqkv_sb[:, :], wq_hi[:, :].bitcast(F32), ALU.subtract).then_inc(wq_ok, 1)
            dve.wait_ge(ld_sig, 16)
            v.tensor_scalar(sig[:, 1:2], sig[:, 0:1], 2.0, None, ALU.mult).then_inc(sig_ok, 1)
            v.tensor_scalar(sig[:, 2:3], sig[:, 0:1], -1.0, None, ALU.mult).then_inc(sig_ok, 1)
            dve.wait_ge(cb_ps, 1)
            dve.wait_ge(ld_bq, 16)
            v.tensor_tensor(cb16[:, :], work[2][0:NB, 0:NQKV], bq16[:, :], ALU.add).then_inc(cb_sb, 1)
            dve.wait_ge(gate_ps, 1)
            gates = scores[0:NB, 3, 0:2 * C].rearrange("b (m c) -> b m c", m=2)
            v.tensor_scalar(g_up[:, :, :], gates, GATE_MIN, None, ALU.max).then_inc(g_step, 1)
            v.tensor_scalar(g_down[:, :, :], gates, -GATE_MIN, None, ALU.min).then_inc(g_step, 1)
            dve.wait_ge(g_step, 2)
            v.scalar_tensor_tensor(g_up[:, :, :], gates, 0.0, g_up[:, :, :], ALU.is_ge, ALU.mult).then_inc(g_step, 1)
            v.scalar_tensor_tensor(g_down[:, :, :], gates, 0.0, g_down[:, :, :], ALU.is_lt, ALU.mult).then_inc(g_step, 1)
            dve.wait_ge(g_step, 4)
            dve.wait_ge(ld_bp, 16)
            v.tensor_tensor(rb16[:, 0:C], g_up[:, 0, :], g_down[:, 0, :], ALU.add).then_inc(g_step, 1)
            v.tensor_tensor(rb16[:, 2 * C:3 * C], g_up[:, 1, :], g_down[:, 1, :], ALU.add).then_inc(gates_ok, 1)
            dve.wait_ge(g_step, 5)
            v.tensor_tensor(rb16[:, C:2 * C], rb16[:, 0:C], bp16[:, :], ALU.mult).then_inc(gates_ok, 1)

            def ln_stats(n, b, bn):
                for t in range(NT):
                    i = v.bn_stats(stats[:, n, t, :], x_all[:, b, t * C:(t + 1) * C])
                i.then_inc(bn, 1)

            def ln_aggregate(n, mv_ok):
                for t in range(NT):
                    i = v.bn_aggr(mv[:, n, t, :], stats[:, n, t, :])
                i.then_inc(mv_ok, 1)

            def normalise(n, dst, b, ready, done):
                dve.wait_ge(ready, b + 1)
                for t in range(NT):
                    i = v.tensor_scalar(dst[:, t * C:(t + 1) * C], x_all[:, b, t * C:(t + 1) * C], mv[:, n, t, 0:1],
                                        rstd[:, n, t:t + 1], ALU.subtract, ALU.mult)
                i.then_inc(done, 1)

            def split_qk(b):
                q2 = qk[:, 0, :, :].rearrange("p t (h d) -> p (t h) d", d=HD)
                k2 = qk[:, 1, :, :].rearrange("p t (h d) -> p (t h) d", d=HD)
                dve.wait_ge(norm_ok, b + 1)
                v.tensor_scalar(norm_rows(0), norms[:, :, :], sig[:, 2:3], None, ALU.mult).then_inc(norm_hi, 1)
                dve.wait_ge(part_k, b + 1)
                v.tensor_tensor(stk_k[:, :, HD:2 * HD], k2, stk_k[:, :, 0:HD].bitcast(F32), ALU.subtract)
                dve.wait_ge(part_q, b + 1)
                v.scalar_tensor_tensor(stk_q[:, :, 2 * HD:3 * HD], q2, sig[:, 1:2], stk_q[:, :, 0:HD].bitcast(F32), ALU.mult, ALU.subtract)
                dve.wait_ge(norm_hi, b + 1)
                v.scalar_tensor_tensor(norm_rows(1), norms[:, :, :], sig[:, 2:3], norm_rows(0).bitcast(F32), ALU.mult, ALU.subtract).then_inc(stk_ok, 1)

            def bias_qk(n, t, bank):
                v.tensor_tensor(qk[:, :, t, :], work[bank][:, 0:2 * C].rearrange("p (a c) -> p a c", a=2),
                                cb_all[:, n, 0:2 * C].rearrange("p (a c) -> p a c", a=2), ALU.add)

            def bias_v(n, q, t, bank):
                v.tensor_tensor(vpad[:, q, t, :, :].rearrange("p r (g w) -> p r g w", g=G)[:, :, :, 0:HD],
                                work[bank][:, 2 * C:3 * C].rearrange("p (g r d) -> p r g d", r=R, g=G),
                                cb_all[:, n, 2 * C:3 * C].rearrange("p (g r d) -> p r g d", r=R, g=G), ALU.add).then_inc(qk_sb, 1)

            def experts(b, q, c, bank):
                dve.wait_ge(f_ps, NC * b + c + 1)
                for e in range(EC):
                    for t in range(NT):
                        j = NT * (EC * c + e) + t
                        if j < NT:
                            dve.wait_ge(acc_init, b + 1)
                        else:
                            dve.wait_ge(acc_step, STEPS * b + j - NT + 1)
                        v.scalar_tensor_tensor(acc[:, q, t, :], work[bank][:, (t * EC + e) * C:(t * EC + e + 1) * C],
                                               mask[:, q, t, 0, EC * c + e:EC * c + e + 1], acc[:, q, t, :],
                                               ALU.mult, ALU.add).then_inc(acc_step, 1)

            def step(k, par):
                odd = (par + 1) % 2
                a, b, c = range(3)
                if has(k + 2):
                    if isinstance(k, int) and k <= 0:
                        dve.wait_ge(*((ld_x0, 16), (ld_x0, 16), (rows_in, 48))[k + 2])
                    elif not isinstance(k, int) or k != 1:
                        wait_apart(dve, rows_in, 48 * k - 48)
                    ln_stats(0, k + 2, ln1_bn)
                    dve.wait_ge(ln1_bn, k + 3)
                if has(k - 3):
                    experts(k - 3, odd, 3, a)
                if has(k + 2):
                    ln_aggregate(0, ln1_mv)
                if has(k - 1):
                    dve.wait_ge(att_hi, k)
                    v.tensor_tensor(o_lo[:, :], att_ps[:, 0:T], o_hi[:, :].bitcast(F32), ALU.subtract).then_inc(att_ok, 1)
                if has(k - 2):
                    dve.wait_ge(h2_hi_ok, k - 1)
                    v.scalar_tensor_tensor(h2_lo[:, par, :], work[b][:, 0:T], col(scale_col[:, 1, :], k - 2), h2_hi[:, par, :].bitcast(F32),
                                           ALU.mult, ALU.subtract).then_inc(h2_ok, 1)
                if has(k + 1):
                    dve.wait_ge(t1_hi, k + 2)
                    v.scalar_tensor_tensor(h1_lo[:, :], work[c][:, 0:T], col(scale_col[:, 0, :], k + 1), h1_hi[:, :].bitcast(F32),
                                           ALU.mult, ALU.subtract).then_inc(t1_ok, 1)
                if has(k - 2):
                    dve.wait_ge(r_ps, k - 1)
                    v.tensor_reduce(logit[:, :, :], work[a][:, 0:NT * 2 * NE].rearrange("p (t i e) -> p t e i", t=NT, i=2), AX.X, ALU.add).then_inc(lsum_ok, 1)
                    dve.wait_ge(lsum_ok, k - 1)
                    v.tensor_tensor(logit[:, :, :], logit[:, :, :], rb_all[:, k - 2, 3 * C:RB].unsqueeze(1).broadcast_to([P, NT, NE]), ALU.add).then_inc(logit_ok, 1)
                    wait_apart(dve, logit_ok, k - 1)
                    for t in range(NT):
                        i = v.max(top[:, t, :], logit[:, t, :])
                    i.then_inc(top_ok, 1)
                if has(k + 1):
                    if isinstance(k, int) and k == -1:
                        dve.wait_ge(ld_cb0, 16)
                        dve.wait_ge(const_ok, 6)
                    dve.wait_ge(qkv_ps, NT * (k + 1) + 1)
                    bias_qk(k + 1, 0, b)
                    bias_v(k + 1, odd, 0, b)
                if has(k - 2):
                    wait_apart(dve, top_ok, k - 1)
                    for t in range(NT):
                        i = v.max_index(topi[:, t, :], top[:, t, :], logit[:, t, :])
                    i.then_inc(topi_ok, 1)
                if has(k + 1):
                    dve.wait_ge(qkv_ps, NT * (k + 1) + 2)
                    bias_qk(k + 1, 1, c)
                    bias_v(k + 1, odd, 1, c)
                if has(k - 2):
                    dve.wait_ge(topi_ok, k - 1)
                    v.tensor_tensor(eq[:, :, :, :], slot_e[:, :, :, :], topi[:, :, 0:2].unsqueeze(3).broadcast_to([P, NT, 2, NE]),
                                    ALU.is_equal).then_inc(eq_ok, 1)
                    dve.wait_ge(eq_ok, k - 1)
                    v.tensor_tensor(mask[:, par, :, :, :], eq[:, :, 0:1, :].broadcast_to([P, NT, 2, NE]),
                                    eq[:, :, 1:2, :].broadcast_to([P, NT, 2, NE]), ALU.add).then_inc(mask_ok, 1)
                if has(k + 2):
                    normalise(0, xn[:, par, :], k + 2, ln1_rstd, xn_ok)
                if has(k - 1):
                    n = k - 1
                    dve.wait_ge(proj_ps, n + 1)
                    dve.wait_ge(xp_ok, n + 1)
                    v.tensor_tensor(x_all[:, n, :], work[b][:, 0:NT * C], x_all[:, n, :], ALU.add).then_inc(x1_ok, 1)
                if has(k - 1):
                    wait_apart(dve, x1_ok, k)
                    ln_stats(1, k - 1, ln2_bn)
                    dve.wait_ge(ln2_bn, k)
                if has(k + 1):
                    dve.wait_ge(sq_ok, k + 2)
                    v.tensor_reduce(norms[:, :, :], sq[:, :, :, :].rearrange("p a t (h d) -> p (a t h) d", d=HD), AX.X, ALU.add).then_inc(norm_ok, 1)
                if has(k + 1):
                    split_qk(k + 1)
                if has(k - 2):
                    experts(k - 2, par, 0, c)
                if has(k - 2):
                    experts(k - 2, par, 1, a)
                if has(k - 1):
                    ln_aggregate(1, ln2_mv)
                if has(k - 2):
                    experts(k - 2, par, 2, b)
                if has(k - 1):
                    normalise(1, x2n[:, odd, :], k - 1, ln2_rstd, x2n_ok)
                if isinstance(k, int) and k == 0:
                    dve.wait_ge(ld_fb, 32)
                    v.tensor_copy(fb_h[:, :, :], fb_f32[:, :, :]).then_inc(fb_h_ok, 1)
                    dve.wait_ge(fb_h_ok, 1)
                    v.scalar_tensor_tensor(fb_all[:, :, :], fb_h[:, :, :].bitcast(F32), lo_rows[:, 0:1], fb_f32[:, :, :],
                                           ALU.mult, ALU.add).then_inc(fb_ok, 1)
                if isinstance(k, int) and k == -1:
                    dve.wait_ge(we_hi_ok, 1)
                    v.tensor_tensor(we_lo[:, :], we_t[:, 0:NE * C], we_hi[:, :].bitcast(F32), ALU.subtract)
                    v.tensor_tensor(wr_parts[:, NE:2 * NE], we_t[:, NE * C:NW], wr_parts[:, 0:NE].bitcast(F32), ALU.subtract).then_inc(we_ok, 1)
                    dve.wait_ge(fb_ps, 1)
                    dve.wait_ge(ld_be, 16)
                    dve.wait_ge(ld_br, 16)
                    for n, w in enumerate((512, 512, NE)):
                        i = v.tensor_tensor(fb16[:, 512 * n:512 * n + w], scores[0:NB, n, 0:w], be16[:, 512 * n:512 * n + w], ALU.add)
                    i.then_inc(fb_sb, 1)
                    dve.wait_ge(fb_sb, 1)
                    dve.wait_ge(gates_ok, 2)
                    v.tensor_copy(rb16[:, 3 * C:RB], fb16[:, NE * C:NW]).then_inc(rb_ok, 1)

            steps(dve, step)

        @block.tensor
        def _(pe):
            pe.wait_ge(ident_ok, 1)
            pe.wait_ge(c_silu, 1)
            pe.transpose(work[0][:, 0:NB], c_sb[:, 1, :], ident[0:NB, 0:NB]).then_inc(ct_ps, 1)
            pe.wait_ge(ct_sb, 1)
            pe.wait_ge(ld_mod, 16)
            for j, m in enumerate((0, 1, 3, 4)):
                i = pe.matmul(work[1][:, j * NB:(j + 1) * NB], w_mod_sb[:, m * C:(m + 1) * C], s_t[:, :], start=True, stop=True)
            i.then_inc(mod_ps, 1)
            for j, m in enumerate((2, 5)):
                i = pe.matmul(scores[0:NB, 3, j * C:(j + 1) * C], s_t[:, :], w_mod_sb[:, m * C:(m + 1) * C], start=True, stop=True)
            i.then_inc(gate_ps, 1)
            pe.wait_ge(mod_sb, 2)
            pe.wait_ge(ld_qkv, 16)
            pe.matmul(work[2][0:NB, 0:NQKV], shift_col[:, 0, :], wqkv_sb[:, :], start=True, stop=True).then_inc(cb_ps, 1)

            def three(dst, a_hi, a_lo, b_hi, b_lo):
                pe.matmul(dst, a_hi, b_hi, start=True, stop=False)
                pe.matmul(dst, a_lo, b_hi, start=False, stop=False)
                return pe.matmul(dst, a_hi, b_lo, start=False, stop=True)

            def expert_weights():
                pe.wait_ge(ld_we, 16)
                pe.wait_ge(ld_wr, 16)
                for e in range(NE):
                    pe.transpose(scores[:, e // 4, (e % 4) * C:(e % 4 + 1) * C], we_sb[:, e, :], ident[:, :])
                pe.transpose(scores[:, 2, 0:NE], wr_sb[:, :], ident[0:NE, 0:NE]).then_inc(wet_ps, 1)
                pe.wait_ge(wet_sb, 1)
                for n, w in enumerate((512, 512, NE)):
                    i = pe.matmul(scores[0:NB, n, 0:w], shift_col[:, 1, :], we_t[:, 512 * n:512 * n + w], start=True, stop=True)
                i.then_inc(fb_ps, 1)

            def warm_up(n):
                for _ in range(n):
                    pe.matmul(att_ps[:, 0:NQKV], wq_hi[:, 0:P], wq_hi[:, :], start=True, stop=True)

            def qk_scores(k, par, g):
                n = 4 * k + g
                pe.wait_ge(st_sb, 4 * k + g + 1)
                if isinstance(k, int) and k == 0 and g == 0:
                    pe.wait_ge(fb_sb, 1)
                for half in range(2):
                    if not isinstance(n, int) or n > 0:
                        pe.wait_ge((exp_a, exp_b)[half], n)
                    for t in range(NT):
                        for r in (2 * half, 2 * half + 1):
                            rows = slice(r * ROWS, (r + 1) * ROWS)
                            i = pe.matmul(scores[:, r, t * T:(t + 1) * T], st_t[rows, par, g, t * P:(t + 1) * P],
                                          st_t[rows, par, g, T:2 * T], start=True, stop=True)
                    i.then_inc((qk_a, qk_b)[half], 1)

            def pv(b, q, g):
                pe.wait_ge(exp_a, 4 * b + g + 1)
                pe.wait_ge(exp_b, 4 * b + g + 1)
                if g == 0:
                    pe.wait_ge(qk_sb, NT * (b + 1))
                    if not isinstance(b, int) or b > 0:
                        pe.wait_ge(att_ok, b)
                for t in range(NT):
                    for r in range(R):
                        i = pe.matmul(att_ps[r * ROWS:(r + 1) * ROWS, 0:T], vpad[:, q, t, r, g * ROWS:(g + 1) * ROWS],
                                      probs[:, g, r, t * T:(t + 1) * T], start=(g == 0 and t == 0), stop=(g == G - 1 and t == NT - 1))
                i.then_inc(pv_done, 1)

            def stack(b, g, bank):
                for a, src in enumerate((stk_q, stk_k)):
                    for t in range(NT):
                        heads = src[:, t * H + g * R:t * H + (g + 1) * R, :].rearrange("p r w -> p (r w)")
                        i = pe.transpose(work[bank][:, a * T + t * P:a * T + (t + 1) * P].bitcast(F32R), heads, ident_r[:, :])
                i.then_inc(st_ps, 1)

            def qkv_tile(t, bank):
                i = three(work[bank][:, 0:NQKV], h1_hi[:, t * P:(t + 1) * P], h1_lo[:, t * P:(t + 1) * P], wq_hi[:, :], wq_lo[:, :])
                i.then_inc(qkv_ps, 1)

            def expert_chunk(b, q, c, bank):
                for t in range(NT):
                    ts = slice(t * P, (t + 1) * P)
                    ws = slice(c * EC * C, (c + 1) * EC * C)
                    i = three(work[bank][:, t * EC * C:(t + 1) * EC * C], h2_hi[:, q, ts], h2_lo[:, q, ts], we_hi[:, ws], we_lo[:, ws])
                i.then_inc(f_ps, 1)

            def step(k, par):
                odd = (par + 1) % 2
                a, b, c = range(3)
                if has(k):
                    qk_scores(k, par, 0)
                if has(k):
                    if has(k - 3):
                        pe.wait_ge(acc_step, STEPS * (k - 3) + 3 * STEPS // NC)
                    elif isinstance(k, int) and k == 2:
                        pe.wait_ge(x1_ok, 1)
                    stack(k, 2, b)
                    pe.wait_ge(st_sb, 4 * k + 1)
                    stack(k, 3, c)
                if has(k - 3):
                    if has(k):
                        pe.wait_ge(st_sb, 4 * k + 2)
                    else:
                        pe.wait_ge(acc_step, STEPS * (k - 3) + 2 * STEPS // NC)
                    expert_chunk(k - 3, odd, 3, a)
                if has(k - 1):
                    pv(k - 1, odd, 3)
                if has(k - 2):
                    pe.wait_ge(x2n_ok, k - 1)
                    if has(k):
                        pe.wait_ge(st_sb, 4 * k + 3)
                    else:
                        pe.wait_ge(acc_step, STEPS * (k - 3) + 3 * STEPS // NC)
                    for t in range(NT):
                        i = pe.transpose(work[b][:, t * P:(t + 1) * P], x2n[:, par, t * C:(t + 1) * C], ident[:, :])
                    i.then_inc(h2_ps, 1)
                if has(k + 1):
                    pe.wait_ge(xn_ok, k + 2)
                    if has(k):
                        pe.wait_ge(st_sb, 4 * k + 4)
                    elif isinstance(k, int) and k == -1:
                        pe.wait_ge(cb_sb, 1)
                    for t in range(NT):
                        i = pe.transpose(work[c][:, t * P:(t + 1) * P], xn[:, odd, t * C:(t + 1) * C], ident[:, :])
                    i.then_inc(t1_ps, 1)
                if has(k):
                    qk_scores(k, par, 1)
                    pv(k, par, 0)
                if has(k - 2):
                    pe.wait_ge(h2_ok, k - 1)
                    if has(k - 3):
                        pe.wait_ge(acc_step, STEPS * (k - 2))
                    else:
                        pe.wait_ge(we_ok, 1)
                    for t in range(NT):
                        dst = work[a][:, 2 * NE * t:2 * NE * (t + 1)]
                        pe.matmul(dst, h2_hi[:, par, t * P:(t + 1) * P], wr_parts[:, :], start=True, stop=False)
                        i = pe.matmul(dst[:, 0:NE], h2_lo[:, par, t * P:(t + 1) * P], wr_parts[:, 0:NE], start=False, stop=True)
                    i.then_inc(r_ps, 1)
                if has(k + 1):
                    pe.wait_ge(t1_ok, k + 2)
                    if isinstance(k, int) and k == -1:
                        pe.wait_ge(wq_ok, 1)
                        pe.wait_ge(ident_r_ok, 1)
                    qkv_tile(0, b)
                    qkv_tile(1, c)
                if has(k):
                    qk_scores(k, par, 2)
                if has(k - 1):
                    pe.wait_ge(att_ok, k)
                    pe.wait_ge(wg_ok, k)
                    if has(k + 1):
                        pe.wait_ge(qk_sb, NT * (k + 1) + 1)
                    for t in range(NT):
                        i = three(work[b][:, t * C:(t + 1) * C], o_hi[:, t * P:(t + 1) * P], o_lo[:, t * P:(t + 1) * P],
                                  wg_hi[:, odd, :], wg_lo[:, odd, :])
                    i.then_inc(proj_ps, 1)
                if has(k - 2):
                    if has(k + 1):
                        pe.wait_ge(qk_sb, NT * (k + 2))
                    elif has(k):
                        pe.wait_ge(st_sb, 4 * k + 4)
                    expert_chunk(k - 2, par, 0, c)
                    pe.wait_ge(mask_ok, k - 1)
                    for t in range(NT):
                        i = pe.transpose(work[a][0:2 * NE, T + t * P:T + (t + 1) * P], mask[:, par, t, :, :].rearrange("p a e -> p (a e)"), ident[:, :])
                    i.then_inc(m_ps, 1)
                if has(k):
                    pv(k, par, 1)
                if has(k - 2):
                    pe.wait_ge(m_sb, k - 1)
                    pe.wait_ge(fbb_ok, k - 1)
                    for t in range(NT):
                        i = pe.matmul(work[a][:, t * C:(t + 1) * C], mask_t[:, t * P:(t + 1) * P], fb_b[:, :], start=True, stop=True)
                    i.then_inc(b_ps, 1)
                if has(k):
                    qk_scores(k, par, 3)
                if has(k - 2):
                    pe.wait_ge(acc_init, k - 1)
                    expert_chunk(k - 2, par, 1, a)
                    if has(k - 1):
                        pe.wait_ge(x1_ok, k)
                    expert_chunk(k - 2, par, 2, b)
                if isinstance(k, int) and k == -1:
                    expert_weights()
                    warm_up(WARM)
                if has(k + 1):
                    pe.wait_ge(stk_ok, k + 2)
                    if has(k - 2):
                        pe.wait_ge(acc_step, STEPS * (k - 2) + STEPS // NC)
                    stack(k + 1, 0, c)
                if has(k):
                    pv(k, par, 2)
                if has(k + 1):
                    if has(k - 2):
                        pe.wait_ge(acc_step, STEPS * (k - 2) + 2 * STEPS // NC)
                    stack(k + 1, 1, a)

            steps(pe, step)


_INS = ['L0_attn_x', 'L0_attn_Wqkv', 'L0_attn_bqkv', 'L0_attn_r_sigma', 'L0_attn_Wproj', 'L0_attn_bproj',
        'L0_ffn_w_router', 'L0_ffn_b_router', 'L0_ffn_w_experts', 'L0_ffn_b_experts', 'L0_c', 'L0_wmod']


def kernel(**inputs):
    import numpy as _np
    import concourse.bacc as _bacc
    from concourse import mybir as _mybir
    from concourse.bass_utils import run_bass_kernel_spmd as _run

    nc = _bacc.Bacc("TRN2", target_bir_lowering=False, num_devices=1)
    arrays, args = {}, []
    for name in _INS:
        a = _np.ascontiguousarray(inputs[name])
        if name == 'L0_attn_r_sigma':
            a = a.reshape(1)
        arrays[f"in_{name}_dram"] = a
        args.append(nc.dram_tensor(f"in_{name}_dram", a.shape, _mybir.dt.from_np(a.dtype), kind="ExternalInput").ap())
    shape = inputs['L0_attn_x'].shape
    args.append(nc.dram_tensor("out_dram", shape, _mybir.dt.float32, kind="ExternalOutput").ap())
    adaln_block(nc, *args)
    r = _run(nc, [arrays], core_ids=[0])
    return r.results[0]["out_dram"]
```

```python
from contextlib import ExitStack

import concourse.bass as bass
from concourse import mybir

F32 = mybir.dt.float32
F32R = mybir.dt.float32r
U32 = mybir.dt.uint32
ALU = mybir.AluOpType
ACT = mybir.ActivationFunctionType
AX = mybir.AxisListType

LN_EPS = 1e-5
GATE_MIN = 0.25
LOOK = 5
WARM = 16
FILL = 2
FILL_END = 2


def adaln_block(nc, x, w_qkv, b_qkv, sigma, w_proj, b_proj, w_router, b_router, w_experts, b_experts, cond, w_mod, out):
    NB, T, C = x.shape
    P = 128
    NT = T // P
    NE = w_router.shape[0]
    HD = 8
    H = C // HD
    R = 4
    G = H // R
    ROWS = P // R
    VBLK = 160
    NC = 4
    EC = NE // NC
    RB = 3 * C + NE
    U = 4
    STEPS = NE * NT
    NP = 4
    NQKV = 3 * C
    NW = NE * C + NE

    xv = x.rearrange("b (p t) c -> b p (t c)", t=NT)
    ov = out.rearrange("b (p t) c -> b p (t c)", t=NT)

    cb_dram = nc.dram_tensor("cb_rows", [NB, NQKV], F32).ap()
    rb_dram = nc.dram_tensor("rb_rows", [NB, RB], F32).ap()
    fb_dram = nc.dram_tensor("fb_rows", [NB, 2, NE * C], F32).ap()

    with ExitStack() as ctx:
        def sb(name, shape, dt=F32):
            return ctx.enter_context(nc.sbuf_tensor(name, shape, dt))

        def sem(name):
            return ctx.enter_context(nc.semaphore(name))

        scores = ctx.enter_context(nc.psum_tensor("scores", [P, R, NT * T], F32))
        att_ps = ctx.enter_context(nc.psum_tensor("att_ps", [P, 512], F32))
        work = [ctx.enter_context(nc.psum_tensor(f"work{i}", [P, 512], F32)) for i in range(3)]

        x_all = sb("x_all", [P, NB, NT * C])
        cb_all = sb("cb_all", [P, NB, NQKV])
        rb_all = sb("rb_all", [P, NB, RB])
        fb_all = sb("fb_all", [2 * NE, NB, C])
        ident = sb("ident", [P, P])
        ident_r = sb("ident_r", [P, P], F32R)
        wq_hi = sb("wq_hi", [P, NQKV], F32R)
        wq_lo = sb("wq_lo", [P, NQKV], F32R)
        we_hi = sb("we_hi", [P, NE * C], F32R)
        we_lo = sb("we_lo", [P, NE * C], F32R)
        wr_parts = sb("wr_parts", [P, 2 * NE], F32R)
        wproj_sb = sb("wproj_sb", [P, C])
        scale_col = sb("scale_col", [P, 2, NB])
        sig = sb("sig", [P, 3])
        expo = sb("expo", [P, NT])
        eps = sb("eps", [P, NT])
        slot_e = sb("slot_e", [P, NT, 2, NE])

        stats = sb("stats", [P, 2, NT, 6])
        mv = sb("mv", [P, 2, NT, 2])
        ve = sb("ve", [P, 2, NT])
        rstd = sb("rstd", [P, 2, NT])
        xn = sb("xn", [P, 2, NT * C])
        h1_hi = sb("h1_hi", [P, T], F32R)
        h1_lo = sb("h1_lo", [P, T], F32R)
        qk = sb("qk", [P, 2, NT, C])
        sq = sb("sq", [P, 2, NT, C])
        norms = sb("norms", [P, 2, NT * H])
        stk = sb("stk", [P, 2 * (NT * H * ROWS + 2)], F32R)
        st_t = sb("st_t", [P, 2, G, 2 * T], F32R)
        vpad = sb("vpad", [P, 2, NT, R, VBLK])
        probs = sb("probs", [P, NP, R, NT * T])
        o_hi = sb("o_hi", [P, T], F32R)
        o_lo = sb("o_lo", [P, T], F32R)
        wg = sb("wg", [P, C])
        wg_hi = sb("wg_hi", [P, 2, C], F32R)
        wg_lo = sb("wg_lo", [P, 2, C], F32R)
        x2n = sb("x2n", [P, 2, NT * C])
        h2_hi = sb("h2_hi", [P, 2, T], F32R)
        h2_lo = sb("h2_lo", [P, 2, T], F32R)
        logit = sb("logit", [P, NT, NE])
        top = sb("top", [P, NT, NE])
        topi = sb("topi", [P, NT, NE], U32)
        eq = sb("eq", [P, NT, 2, NE])
        mask = sb("mask", [P, 2, NT, 2, NE], F32R)
        mask_t = sb("mask_t", [2 * NE, T], F32R)
        fb_b = sb("fb_b", [2 * NE, C], F32R)
        acc = sb("acc", [P, 2, NT, C])
        gated = sb("gated", [P, NT * C])

        spare = probs[:, :, :, :].rearrange("p a r n -> p (a r n)")
        w_mod_sb = spare[:, 0:6 * C]
        wqkv_sb = sb("wqkv_sb", [P, NQKV])
        wr_sb = sb("wr_sb", [NE, C])
        we_sb = spare[:, 1024:1024 + NE * C].rearrange("p (e c) -> p e c", e=NE)
        we_t = spare[:, 2048:2048 + NW]
        c_sb = sb("c_sb", [NB, 3, C])
        s_t = sb("s_t", [P, NB])
        shift_col = sb("shift_col", [P, 2, NB])
        bq16 = sb("bq16", [NB, NQKV])
        bp16 = sb("bp16", [NB, C])
        be16 = spare[0:NB, 4096:4096 + NW]
        cb16 = sb("cb16", [NB, NQKV])
        rb16 = sb("rb16", [NB, RB])
        fb16 = sb("fb16", [NB, NW])
        g_up = sb("g_up", [NB, 2, C])
        g_down = sb("g_down", [NB, 2, C])
        fb_parts = sb("fb_parts", [NB, 2, NE * C], F32R)

        ld_c = sem("ld_c")
        ld_mod = sem("ld_mod")
        ld_qkv = sem("ld_qkv")
        ld_x0 = sem("ld_x0")
        ld_bq = sem("ld_bq")
        ld_bp = sem("ld_bp")
        ld_sig = sem("ld_sig")
        ld_x1 = sem("ld_x1")
        ld_rb = sem("ld_rb")
        rows_in = sem("rows_in")
        ld_we = sem("ld_we")
        ld_wr = sem("ld_wr")
        ld_be = sem("ld_be")
        ld_br = sem("ld_br")
        ld_proj = sem("ld_proj")
        st_cb = sem("st_cb")
        st_rb = sem("st_rb")
        st_fb = sem("st_fb")
        ld_cb0 = sem("ld_cb0")
        ld_cb1 = sem("ld_cb1")
        ld_fb = sem("ld_fb")
        stored = sem("stored")
        ident_z = sem("ident_z")
        ident_ok = sem("ident_ok")
        ident_r_ok = sem("ident_r_ok")
        const_ok = sem("const_ok")
        expo_ok = sem("expo_ok")
        c_exp = sem("c_exp")
        c_den = sem("c_den")
        c_rec = sem("c_rec")
        c_silu = sem("c_silu")
        ct_ps = sem("ct_ps")
        ct_sb = sem("ct_sb")
        mod_ps = sem("mod_ps")
        gate_ps = sem("gate_ps")
        mod_sb = sem("mod_sb")
        cb_ps = sem("cb_ps")
        cb_sb = sem("cb_sb")
        sig_ok = sem("sig_ok")
        g_step = sem("g_step")
        gates_ok = sem("gates_ok")
        wq_hi_ok = sem("wq_hi_ok")
        wq_ok = sem("wq_ok")
        wet_ps = sem("wet_ps")
        wet_sb = sem("wet_sb")
        we_hi_ok = sem("we_hi_ok")
        we_ok = sem("we_ok")
        fb_ps = sem("fb_ps")
        fb_raw = sem("fb_raw")
        fb_sb = sem("fb_sb")
        rb_ok = sem("rb_ok")
        fb_hi_ok = sem("fb_hi_ok")
        fb_lo_ok = sem("fb_lo_ok")
        ln1_bn = sem("ln1_bn")
        ln1_mv = sem("ln1_mv")
        ln1_ve = sem("ln1_ve")
        ln1_rstd = sem("ln1_rstd")
        xn_ok = sem("xn_ok")
        t1_ps = sem("t1_ps")
        t1_hi = sem("t1_hi")
        t1_ok = sem("t1_ok")
        qkv_ps = sem("qkv_ps")
        qk_sb = sem("qk_sb")
        sq_ok = sem("sq_ok")
        norm_ok = sem("norm_ok")
        part_k = sem("part_k")
        part_q = sem("part_q")
        norm_hi = sem("norm_hi")
        stk_ok = sem("stk_ok")
        st_ps = sem("st_ps")
        st_sb = sem("st_sb")
        qk_a = sem("qk_a")
        qk_b = sem("qk_b")
        exp_a = sem("exp_a")
        exp_b = sem("exp_b")
        pv_done = sem("pv_done")
        att_hi = sem("att_hi")
        att_ok = sem("att_ok")
        wg_h = sem("wg_h")
        wg_ok = sem("wg_ok")
        xp_ok = sem("xp_ok")
        proj_ps = sem("proj_ps")
        x1_ok = sem("x1_ok")
        ln2_bn = sem("ln2_bn")
        ln2_mv = sem("ln2_mv")
        ln2_ve = sem("ln2_ve")
        ln2_rstd = sem("ln2_rstd")
        x2n_ok = sem("x2n_ok")
        h2_ps = sem("h2_ps")
        h2_hi_ok = sem("h2_hi_ok")
        h2_ok = sem("h2_ok")
        r_ps = sem("r_ps")
        lsum_ok = sem("lsum_ok")
        logit_ok = sem("logit_ok")
        top_ok = sem("top_ok")
        topi_ok = sem("topi_ok")
        eq_ok = sem("eq_ok")
        mask_ok = sem("mask_ok")
        m_ps = sem("m_ps")
        m_sb = sem("m_sb")
        fbb_ok = sem("fbb_ok")
        b_ps = sem("b_ps")
        acc_init = sem("acc_init")
        f_ps = sem("f_ps")
        acc_step = sem("acc_step")
        gated_ok = sem("gated_ok")
        res_ok = sem("res_ok")

        stk_q = stk[:, 0:NT * H * ROWS].rearrange("p (h w) -> p h w", w=ROWS)
        stk_k = stk[:, NT * H * ROWS:2 * NT * H * ROWS].rearrange("p (h w) -> p h w", w=ROWS)
        stk_qk = stk[:, :].rearrange("p (a n) -> p a n", a=2)
        NQ = 3 * HD

        def norm_rows(i):
            return stk_qk[:, :, NQ + i:NQ + i + (NT * H - 1) * ROWS + 1:ROWS]

        hi_rows_q = stk_q[:, :, 0:2 * HD].rearrange("p h (i d) -> p h i d", i=2)
        hi_rows_k = stk_k[:, :, :].rearrange("p h (i d) -> p h i d", i=2)[:, :, :, 0:HD]

        def twice(a):
            return qk[:, a, :, :].rearrange("p t (h d) -> p (t h) d", d=HD).unsqueeze(2).broadcast_to([P, NT * H, 2, HD])

        block = ctx.enter_context(nc.Block())

        def has(b):
            return not isinstance(b, int) or 0 <= b < NB

        def steps(eng, step):
            for k in range(-2, U):
                step(k, k % 2)
            with eng.Fori(1, NB // U - 1, 1) as i:
                for u in range(U):
                    step(U * i + u, u % 2)
            for k in range(NB - U, NB + 3):
                step(k, k % 2)

        def banks(k):
            if isinstance(k, int) and k == NB + 1:
                return [scores[:, i, :] for i in range(R)]
            return work[0][:, :], work[1][:, :], work[2][:, :], work[0][:, :]

        def wait_apart(eng, semaphore, value):
            eng.wait_ge(ident_ok, 1)
            eng.wait_ge(semaphore, value)

        def col(t, b):
            return t[:, bass.ds(b, 1)]

        @block.sync
        def _(sp):
            sp.dma_start(c_sb[:, 0, :], cond).then_inc(ld_c, 16)
            sp.dma_start(w_mod_sb[:, :], w_mod).then_inc(ld_mod, 16)
            sp.dma_start(x_all[:, 0:2, :], xv[0:2].rearrange("b p n -> p b n")).then_inc(ld_x0, 16)
            sp.dma_start(wqkv_sb[:, :], w_qkv).then_inc(ld_qkv, 16)
            sp.dma_start(we_sb[:, :, :], w_experts.rearrange("e o d -> o e d")).then_inc(ld_we, 16)
            sp.dma_start(wr_sb[:, :], w_router).then_inc(ld_wr, 16)
            sp.dma_start(bq16[:, :], b_qkv.partition_broadcast(NB)).then_inc(ld_bq, 16)
            sp.dma_start(sig[:, 0:1], sigma.partition_broadcast(P)).then_inc(ld_sig, 16)
            sp.dma_start(be16[:, 0:NE * C], b_experts.rearrange("e o -> (e o)").partition_broadcast(NB)).then_inc(ld_be, 16)
            sp.dma_start(be16[:, NE * C:NW], b_router.partition_broadcast(NB)).then_inc(ld_br, 16)
            sp.dma_start(bp16[:, :], b_proj.partition_broadcast(NB)).then_inc(ld_bp, 16)
            sp.wait_ge(cb_sb, 1)
            sp.dma_start(cb_dram, cb16[:, :]).then_inc(st_cb, 16)
            sp.wait_ge(st_cb, 16)
            sp.dma_start(cb_all[:, 0:1, :], cb_dram[0:1].partition_broadcast(P)).then_inc(ld_cb0, 16)
            sp.dma_start(x_all[:, 2:LOOK, :], xv[2:LOOK].rearrange("b p n -> p b n")).then_inc(ld_x1, 16)
            sp.dma_start(cb_all[:, 1:LOOK, :], cb_dram[1:LOOK].partition_broadcast(P)).then_inc(ld_cb1, 16)
            for r in range(R):
                sp.dma_start(wproj_sb[r * ROWS:(r + 1) * ROWS, :],
                             w_proj.rearrange("(g r d) n -> r g d n", g=G, r=R)[r]).then_inc(ld_proj, 16)
            sp.wait_ge(rb_ok, 1)
            sp.wait_ge(gates_ok, 2)
            sp.dma_start(rb_dram, rb16[:, :]).then_inc(st_rb, 16)
            sp.wait_ge(st_rb, 16)
            sp.dma_start(rb_all[:, 0:LOOK, :], rb_dram[0:LOOK].partition_broadcast(P)).then_inc(ld_rb, 16)
            sp.wait_ge(fb_lo_ok, 1)
            sp.dma_start(fb_dram, fb_parts[:, :, :].bitcast(F32)).then_inc(st_fb, 16)
            sp.wait_ge(st_fb, 16)
            for half in range(2):
                sp.dma_start(fb_all[half * NE:(half + 1) * NE, :, :],
                             fb_dram[:, half, :].rearrange("b (e o) -> e b o", e=NE)).then_inc(ld_fb, 16)

            def load(n):
                sp.dma_start(x_all[:, n, :], xv[n]).then_inc(rows_in, 16)
                sp.dma_start(cb_all[:, n, :], cb_dram[n].partition_broadcast(P)).then_inc(rows_in, 16)
                sp.dma_start(rb_all[:, n, :], rb_dram[n].partition_broadcast(P)).then_inc(rows_in, 16)

            def store(b):
                sp.wait_ge(res_ok, b + 1)
                sp.dma_start(ov[b], x_all[:, b, :]).then_inc(stored, 16)

            load(LOOK)
            with sp.Fori(0, NB - LOOK - 1, 1) as b:
                sp.wait_ge(rows_in, 48 * b + 48)
                load(b + LOOK + 1)
                store(b)
            with sp.Fori(NB - LOOK - 1, NB, 1) as b:
                store(b)
            sp.wait_ge(stored, 16 * NB)

        @block.gpsimd
        def _(pool):
            nc.gpsimd.memset(ident[:, :], 0.0).then_inc(ident_z, 1)
            pool.wait_ge(ident_z, 1)
            nc.gpsimd.affine_select(out=ident[:, :], in_=ident[:, :], compare_op=ALU.not_equal, fill=1.0, base=0,
                                    pattern=[[-1, P]], channel_multiplier=1).then_inc(ident_ok, 1)
            nc.gpsimd.memset(expo[:, :], -0.5).then_inc(expo_ok, 1)
            nc.gpsimd.memset(eps[:, :], LN_EPS).then_inc(expo_ok, 1)
            nc.gpsimd.memset(stk[:, :].bitcast(F32), 0.0).then_inc(const_ok, 1)
            nc.gpsimd.memset(vpad[:, :, :, :, :].rearrange("p a t r n -> p (a t r n)"), 0.0).then_inc(const_ok, 1)
            nc.gpsimd.iota(slot_e[:, :, :, :], [[0, NT], [0, 2], [1, NE]], base=0, channel_multiplier=0,
                           allow_small_or_imprecise_dtypes=True).then_inc(const_ok, 1)
            pool.wait_ge(const_ok, 3)
            nc.gpsimd.memset(stk_q[:, :, NQ + 2:NQ + 4].bitcast(F32), 1.0).then_inc(const_ok, 1)
            nc.gpsimd.memset(stk_k[:, :, NQ:NQ + 2].bitcast(F32), 1.0).then_inc(const_ok, 1)

            def rsqrt(n, b, bn, ve_ok, done):
                wait_apart(pool, bn, b + 1)
                nc.gpsimd.tensor_tensor(ve[:, n, :], mv[:, n, :, 1], eps[:, :], ALU.add).then_inc(ve_ok, 1)
                wait_apart(pool, ve_ok, b + 1)
                nc.gpsimd.tensor_tensor(rstd[:, n, :], ve[:, n, :], expo[:, :], ALU.pow).then_inc(done, 1)

            def step(k, par):
                odd = (par + 1) % 2
                if has(k + 2):
                    rsqrt(0, k + 2, ln1_mv, ln1_ve, ln1_rstd)
                if has(k - 2):
                    b = k - 2
                    if has(k - 3):
                        wait_apart(pool, b_ps, b)
                    else:
                        pool.wait_ge(ld_fb, 32)
                    nc.gpsimd.tensor_copy(fb_b[:, :], fb_all[:, b, :]).then_inc(fbb_ok, 1)
                if has(k - 1):
                    b = k - 1
                    if has(k - 2):
                        wait_apart(pool, wg_ok, b)
                    else:
                        pool.wait_ge(ld_rb, 16)
                        pool.wait_ge(ld_proj, 16 * R)
                    nc.gpsimd.tensor_tensor(wg[:, :], wproj_sb[:, :], rb_all[:, b, 0:C], ALU.mult)
                    nc.gpsimd.tensor_tensor(wg_hi[:, odd, :], wproj_sb[:, :], rb_all[:, b, 0:C], ALU.mult).then_inc(wg_h, 1)
                    wait_apart(pool, wg_h, b + 1)
                    nc.gpsimd.tensor_tensor(wg_lo[:, odd, :], wg[:, :], wg_hi[:, odd, :].bitcast(F32), ALU.subtract).then_inc(wg_ok, 1)
                    for t in range(NT):
                        xs = x_all[:, b, t * C:(t + 1) * C]
                        i = nc.gpsimd.tensor_tensor(xs, xs, rb_all[:, b, C:2 * C], ALU.add)
                    i.then_inc(xp_ok, 1)
                if has(k + 1):
                    b = k + 1
                    for t in range(NT):
                        pool.wait_ge(qk_sb, NT * b + t + 1)
                        i = nc.gpsimd.tensor_tensor(sq[:, :, t, :], qk[:, :, t, :], qk[:, :, t, :], ALU.mult)
                    i.then_inc(sq_ok, 1)
                if has(k - 3) and has(k - 2):
                    b = k - 3
                    wait_apart(pool, acc_step, STEPS * (b + 1))
                    if not has(k - 1):
                        pool.wait_ge(res_ok, b)
                    for t in range(NT):
                        i = nc.gpsimd.tensor_tensor(gated[:, t * C:(t + 1) * C], acc[:, odd, t, :], rb_all[:, b, 2 * C:3 * C], ALU.mult)
                    i.then_inc(gated_ok, 1)
                    wait_apart(pool, gated_ok, b + 1)
                    nc.gpsimd.tensor_tensor(x_all[:, b, :], x_all[:, b, :], gated[:, :], ALU.add).then_inc(res_ok, 1)
                if has(k - 1):
                    rsqrt(1, k - 1, ln2_mv, ln2_ve, ln2_rstd)

            steps(pool, step)

        @block.scalar
        def _(act):
            act.wait_ge(ld_c, 16)
            nc.scalar.activation(c_sb[:, 1, :], c_sb[:, 0, :], ACT.Exp, scale=-1.0).then_inc(c_exp, 1)
            act.wait_ge(ld_qkv, 16)
            nc.scalar.copy(wq_hi[:, :], wqkv_sb[:, :]).then_inc(wq_hi_ok, 1)

            def expert_weights():
                act.wait_ge(wet_ps, 1)
                nc.scalar.copy(we_t[:, 0:2 * 512], scores[:, 0:2, :].rearrange("p r n -> p (r n)"))
                nc.scalar.copy(we_t[:, NE * C:NW], scores[:, 2, 0:NE]).then_inc(wet_sb, 1)

            def exp(k, g, half):
                n = 4 * k + g
                done = (exp_a, exp_b)[half]
                act.wait_ge((qk_a, qk_b)[half], n + 1)
                if not isinstance(n, int) or n >= NP:
                    act.wait_ge(pv_done, n - NP + 1)
                nc.scalar.activation(probs[:, g, 2 * half:2 * half + 2, :], scores[:, 2 * half:2 * half + 2, :], ACT.Exp).then_inc(done, 1)

            def stack_out(b, q, g, bank):
                act.wait_ge(st_ps, 4 * b + g + 1)
                nc.scalar.copy(st_t[:, q, g, :], bank[:, :]).then_inc(st_sb, 1)

            def step(k, par):
                odd = (par + 1) % 2
                a, b, c, router = banks(k)
                if has(k):
                    exp(k, 0, 0)
                    stack_out(k, par, 2, b)
                    stack_out(k, par, 3, c)
                    exp(k, 0, 1)
                if has(k - 1):
                    act.wait_ge(pv_done, 4 * k)
                    nc.scalar.copy(o_hi[:, :], att_ps[:, 0:T]).then_inc(att_hi, 1)
                if has(k - 2):
                    act.wait_ge(h2_ps, k - 1)
                    nc.scalar.activation(h2_hi[:, par, :], b[:, 0:T], ACT.Identity, scale=col(scale_col[:, 1, :], k - 2)).then_inc(h2_hi_ok, 1)
                if has(k + 1):
                    act.wait_ge(t1_ps, k + 2)
                    if isinstance(k, int) and k == -1:
                        act.wait_ge(mod_sb, 2)
                    nc.scalar.activation(h1_hi[:, :], c[:, 0:T], ACT.Identity, scale=col(scale_col[:, 0, :], k + 1)).then_inc(t1_hi, 1)
                if isinstance(k, int) and k == -1:
                    expert_weights()
                if isinstance(k, int) and k == 0:
                    act.wait_ge(we_ok, 1)
                if has(k):
                    exp(k, 1, 0)
                    exp(k, 1, 1)
                if isinstance(k, int) and k == 0:
                    act.wait_ge(fb_sb, 1)
                    nc.scalar.copy(fb_parts[:, 0, :], fb16[:, 0:NE * C]).then_inc(fb_hi_ok, 1)
                if has(k):
                    exp(k, 2, 0)
                if isinstance(k, int) and k == -1:
                    act.wait_ge(fb_ps, 1)
                    nc.scalar.copy(fb16[:, 0:NE * C], scores[0:NB, 0:2, :].rearrange("b r n -> b (r n)"))
                    nc.scalar.copy(fb16[:, NE * C:NW], scores[0:NB, 2, 0:NE]).then_inc(fb_raw, 1)
                if has(k + 1):
                    n = k + 1
                    if has(k):
                        act.wait_ge(st_ps, 4 * n)
                    elif isinstance(k, int) and k == -1:
                        act.wait_ge(sig_ok, 2)
                        act.wait_ge(const_ok, 5)
                    act.wait_ge(qk_sb, NT * (n + 1))
                    nc.scalar.copy(hi_rows_k, twice(1)).then_inc(part_k, 1)
                    nc.scalar.activation(hi_rows_q, twice(0), ACT.Identity, scale=sig[:, 1:2]).then_inc(part_q, 1)
                if has(k - 2):
                    act.wait_ge(m_ps, k - 1)
                    nc.scalar.copy(mask_t[:, :], router[0:2 * NE, T:2 * T]).then_inc(m_sb, 1)
                if has(k):
                    exp(k, 2, 1)
                if has(k - 2):
                    act.wait_ge(b_ps, k - 1)
                    nc.scalar.copy(acc[:, par, :, :].rearrange("p t c -> p (t c)"), router[:, 0:NT * C]).then_inc(acc_init, 1)
                if has(k):
                    exp(k, 3, 0)
                    exp(k, 3, 1)
                if isinstance(k, int) and k == -1:
                    act.wait_ge(wet_sb, 1)
                    nc.scalar.copy(we_hi[:, :], we_t[:, 0:NE * C])
                    nc.scalar.copy(wr_parts[:, 0:NE], we_t[:, NE * C:NW]).then_inc(we_hi_ok, 1)
                if has(k + 1):
                    stack_out(k + 1, odd, 0, c)
                    stack_out(k + 1, odd, 1, a)

            steps(act, step)

        @block.vector
        def _(dve):
            v = nc.vector
            def silu():
                dve.wait_ge(c_exp, 1)
                v.tensor_scalar(c_sb[:, 1, :], c_sb[:, 1, :], 1.0, None, ALU.add).then_inc(c_den, 1)
                dve.wait_ge(c_den, 1)
                v.reciprocal(c_sb[:, 2, :], c_sb[:, 1, :]).then_inc(c_rec, 1)
                dve.wait_ge(c_rec, 1)
                v.tensor_tensor(c_sb[:, 1, :], c_sb[:, 0, :], c_sb[:, 2, :], ALU.mult).then_inc(c_silu, 1)
                dve.wait_ge(ct_ps, 1)
                v.tensor_copy(s_t[:, :], work[0][:, 0:NB]).then_inc(ct_sb, 1)
                v.tensor_copy(ident_r[:, :], ident[:, :]).then_inc(ident_r_ok, 1)

            def modulation():
                dve.wait_ge(mod_ps, 1)
                mod_cols = work[1][:, 0:4 * NB].rearrange("p (m b) -> p m b", m=4)
                v.tensor_copy(shift_col[:, :, :], mod_cols[:, 0:4:2, :]).then_inc(mod_sb, 1)
                v.tensor_scalar(scale_col[:, :, :], mod_cols[:, 1:4:2, :], 1.0, None, ALU.add).then_inc(mod_sb, 1)
                dve.wait_ge(wq_hi_ok, 1)
                v.tensor_tensor(wq_lo[:, :], wqkv_sb[:, :], wq_hi[:, :].bitcast(F32), ALU.subtract).then_inc(wq_ok, 1)
                dve.wait_ge(ld_sig, 16)
                v.tensor_scalar(sig[:, 1:2], sig[:, 0:1], 2.0, None, ALU.mult).then_inc(sig_ok, 1)
                v.tensor_scalar(sig[:, 2:3], sig[:, 0:1], -1.0, None, ALU.mult).then_inc(sig_ok, 1)
                dve.wait_ge(cb_ps, 1)
                dve.wait_ge(ld_bq, 16)
                v.tensor_tensor(cb16[:, :], att_ps[0:NB, 0:NQKV], bq16[:, :], ALU.add).then_inc(cb_sb, 1)

            def gate_rows():
                dve.wait_ge(gate_ps, 1)
                gates = scores[0:NB, 3, 0:2 * C].rearrange("b (m c) -> b m c", m=2)
                v.tensor_scalar(g_up[:, :, :], gates, GATE_MIN, None, ALU.max).then_inc(g_step, 1)
                v.tensor_scalar(g_down[:, :, :], gates, -GATE_MIN, None, ALU.min).then_inc(g_step, 1)
                dve.wait_ge(g_step, 2)
                v.scalar_tensor_tensor(g_up[:, :, :], gates, 0.0, g_up[:, :, :], ALU.is_ge, ALU.mult).then_inc(g_step, 1)
                v.scalar_tensor_tensor(g_down[:, :, :], gates, 0.0, g_down[:, :, :], ALU.is_lt, ALU.mult).then_inc(g_step, 1)
                dve.wait_ge(g_step, 4)
                dve.wait_ge(ld_bp, 16)
                v.tensor_tensor(rb16[:, 0:C], g_up[:, 0, :], g_down[:, 0, :], ALU.add).then_inc(g_step, 1)
                v.tensor_tensor(rb16[:, 2 * C:3 * C], g_up[:, 1, :], g_down[:, 1, :], ALU.add).then_inc(gates_ok, 1)
                dve.wait_ge(g_step, 5)
                v.tensor_tensor(rb16[:, C:2 * C], rb16[:, 0:C], bp16[:, :], ALU.mult).then_inc(gates_ok, 1)

            def ln_stats(n, b, bn):
                for t in range(NT):
                    i = v.bn_stats(stats[:, n, t, :], x_all[:, b, t * C:(t + 1) * C])
                i.then_inc(bn, 1)

            def ln_aggregate(n, mv_ok):
                for t in range(NT):
                    i = v.bn_aggr(mv[:, n, t, :], stats[:, n, t, :])
                i.then_inc(mv_ok, 1)

            def normalise(n, dst, b, ready, done):
                dve.wait_ge(ready, b + 1)
                for t in range(NT):
                    i = v.tensor_scalar(dst[:, t * C:(t + 1) * C], x_all[:, b, t * C:(t + 1) * C], mv[:, n, t, 0:1],
                                        rstd[:, n, t:t + 1], ALU.subtract, ALU.mult)
                i.then_inc(done, 1)

            def split_qk(b):
                q2 = qk[:, 0, :, :].rearrange("p t (h d) -> p (t h) d", d=HD)
                k2 = qk[:, 1, :, :].rearrange("p t (h d) -> p (t h) d", d=HD)
                dve.wait_ge(norm_ok, b + 1)
                v.tensor_scalar(norm_rows(0), norms[:, :, :], sig[:, 2:3], None, ALU.mult).then_inc(norm_hi, 1)
                dve.wait_ge(part_k, b + 1)
                v.tensor_tensor(stk_k[:, :, HD:2 * HD], k2, stk_k[:, :, 0:HD].bitcast(F32), ALU.subtract)
                dve.wait_ge(part_q, b + 1)
                v.scalar_tensor_tensor(stk_q[:, :, 2 * HD:3 * HD], q2, sig[:, 1:2], stk_q[:, :, 0:HD].bitcast(F32), ALU.mult, ALU.subtract)
                dve.wait_ge(norm_hi, b + 1)
                v.scalar_tensor_tensor(norm_rows(1), norms[:, :, :], sig[:, 2:3], norm_rows(0).bitcast(F32), ALU.mult, ALU.subtract).then_inc(stk_ok, 1)

            def bias_qk(n, t, bank):
                v.tensor_tensor(qk[:, :, t, :], bank[:, 0:2 * C].rearrange("p (a c) -> p a c", a=2),
                                cb_all[:, n, 0:2 * C].rearrange("p (a c) -> p a c", a=2), ALU.add)

            def bias_v(n, q, t, bank):
                v.tensor_tensor(vpad[:, q, t, :, :].rearrange("p r (g w) -> p r g w", g=G)[:, :, :, 0:HD],
                                bank[:, 2 * C:3 * C].rearrange("p (g r d) -> p r g d", r=R, g=G),
                                cb_all[:, n, 2 * C:3 * C].rearrange("p (g r d) -> p r g d", r=R, g=G), ALU.add).then_inc(qk_sb, 1)

            def experts(b, q, c, bank):
                dve.wait_ge(f_ps, NC * b + c + 1)
                for e in range(EC):
                    for t in range(NT):
                        j = NT * (EC * c + e) + t
                        if j < NT:
                            dve.wait_ge(acc_init, b + 1)
                        else:
                            dve.wait_ge(acc_step, STEPS * b + j - NT + 1)
                        v.scalar_tensor_tensor(acc[:, q, t, :], bank[:, (t * EC + e) * C:(t * EC + e + 1) * C],
                                               mask[:, q, t, 0, EC * c + e:EC * c + e + 1].bitcast(F32), acc[:, q, t, :],
                                               ALU.mult, ALU.add).then_inc(acc_step, 1)

            def step(k, par):
                odd = (par + 1) % 2
                a, b, c, router = banks(k)
                if isinstance(k, int) and k == -2:
                    silu()
                if has(k + 2):
                    if isinstance(k, int) and k + 2 < LOOK:
                        dve.wait_ge((ld_x0, ld_x1)[k >= 0], 16)
                    else:
                        wait_apart(dve, rows_in, 48 * k - 48 * (LOOK - 3))
                    ln_stats(0, k + 2, ln1_bn)
                    dve.wait_ge(ln1_bn, k + 3)
                alone = isinstance(k, int) and k == NB + 1
                if has(k - 3) and not alone:
                    experts(k - 3, odd, 3, a)
                if has(k - 3) and not has(k - 2):
                    n = k - 3
                    dve.wait_ge(acc_step, STEPS * (n + 1))
                    dve.wait_ge(res_ok, n)
                    for t in range(NT):
                        i = v.tensor_tensor(gated[:, t * C:(t + 1) * C], acc[:, odd, t, :], rb_all[:, n, 2 * C:3 * C], ALU.mult)
                    i.then_inc(gated_ok, 1)
                    dve.wait_ge(gated_ok, n + 1)
                    v.tensor_tensor(x_all[:, n, :], x_all[:, n, :], gated[:, :], ALU.add).then_inc(res_ok, 1)
                if has(k + 2):
                    ln_aggregate(0, ln1_mv)
                if has(k - 1):
                    dve.wait_ge(att_hi, k)
                    v.tensor_tensor(o_lo[:, :], att_ps[:, 0:T], o_hi[:, :].bitcast(F32), ALU.subtract).then_inc(att_ok, 1)
                if has(k - 2):
                    dve.wait_ge(h2_hi_ok, k - 1)
                    v.scalar_tensor_tensor(h2_lo[:, par, :], b[:, 0:T], col(scale_col[:, 1, :], k - 2), h2_hi[:, par, :].bitcast(F32),
                                           ALU.mult, ALU.subtract).then_inc(h2_ok, 1)
                if alone:
                    experts(k - 3, odd, 2, work[1])
                if has(k + 1):
                    dve.wait_ge(t1_hi, k + 2)
                    v.scalar_tensor_tensor(h1_lo[:, :], c[:, 0:T], col(scale_col[:, 0, :], k + 1), h1_hi[:, :].bitcast(F32),
                                           ALU.mult, ALU.subtract).then_inc(t1_ok, 1)
                if isinstance(k, int) and k == -1:
                    gate_rows()
                if has(k - 2):
                    dve.wait_ge(r_ps, k - 1)
                    if isinstance(k, int) and k == 2:
                        dve.wait_ge(ld_rb, 16)
                    v.tensor_reduce(logit[:, :, :], router[:, 0:NT * 2 * NE].rearrange("p (t i e) -> p t e i", t=NT, i=2), AX.X, ALU.add).then_inc(lsum_ok, 1)
                    dve.wait_ge(lsum_ok, k - 1)
                    v.tensor_tensor(logit[:, :, :], logit[:, :, :], rb_all[:, k - 2, 3 * C:RB].unsqueeze(1).broadcast_to([P, NT, NE]), ALU.add).then_inc(logit_ok, 1)
                    wait_apart(dve, logit_ok, k - 1)
                    for t in range(NT):
                        i = v.max(top[:, t, :], logit[:, t, :])
                    i.then_inc(top_ok, 1)
                if has(k + 1):
                    if isinstance(k, int) and k <= 0:
                        dve.wait_ge((ld_cb0, ld_cb1)[k + 1], 16)
                    if isinstance(k, int) and k == -1:
                        dve.wait_ge(const_ok, 5)
                    dve.wait_ge(qkv_ps, NT * (k + 1) + 1)
                    bias_qk(k + 1, 0, b)
                    bias_v(k + 1, odd, 0, b)
                if has(k - 2):
                    wait_apart(dve, top_ok, k - 1)
                    for t in range(NT):
                        i = v.max_index(topi[:, t, :], top[:, t, :], logit[:, t, :])
                    i.then_inc(topi_ok, 1)
                if has(k + 1):
                    dve.wait_ge(qkv_ps, NT * (k + 1) + 2)
                    bias_qk(k + 1, 1, c)
                    bias_v(k + 1, odd, 1, c)
                if has(k - 2):
                    dve.wait_ge(topi_ok, k - 1)
                    v.tensor_tensor(eq[:, :, :, :], slot_e[:, :, :, :], topi[:, :, 0:2].unsqueeze(3).broadcast_to([P, NT, 2, NE]),
                                    ALU.is_equal).then_inc(eq_ok, 1)
                    dve.wait_ge(eq_ok, k - 1)
                    v.tensor_tensor(mask[:, par, :, :, :], eq[:, :, 0:1, :].broadcast_to([P, NT, 2, NE]),
                                    eq[:, :, 1:2, :].broadcast_to([P, NT, 2, NE]), ALU.add).then_inc(mask_ok, 1)
                if alone:
                    experts(k - 3, odd, 3, work[2])
                if has(k + 2):
                    normalise(0, xn[:, par, :], k + 2, ln1_rstd, xn_ok)
                if isinstance(k, int) and k == -2:
                    modulation()
                if has(k - 1):
                    n = k - 1
                    dve.wait_ge(proj_ps, n + 1)
                    dve.wait_ge(xp_ok, n + 1)
                    v.tensor_tensor(x_all[:, n, :], b[:, 0:NT * C], x_all[:, n, :], ALU.add).then_inc(x1_ok, 1)
                if has(k + 1):
                    dve.wait_ge(sq_ok, k + 2)
                    v.tensor_reduce(norms[:, :, :], sq[:, :, :, :].rearrange("p a t (h d) -> p (a t h) d", d=HD), AX.X, ALU.add).then_inc(norm_ok, 1)
                if has(k - 1):
                    wait_apart(dve, x1_ok, k)
                    ln_stats(1, k - 1, ln2_bn)
                    dve.wait_ge(ln2_bn, k)
                    if not has(k):
                        ln_aggregate(1, ln2_mv)
                if has(k + 1):
                    split_qk(k + 1)
                if has(k - 2):
                    experts(k - 2, par, 0, c)
                if has(k - 2) and has(k):
                    experts(k - 2, par, 1, a)
                if has(k - 1) and has(k):
                    ln_aggregate(1, ln2_mv)
                if has(k - 2) and has(k):
                    experts(k - 2, par, 2, b)
                if has(k - 1):
                    normalise(1, x2n[:, odd, :], k - 1, ln2_rstd, x2n_ok)
                if has(k - 2) and not has(k):
                    experts(k - 2, par, 1, a)
                    if alone:
                        experts(k - 2, par, 2, b)
                if isinstance(k, int) and k == 0:
                    dve.wait_ge(fb_hi_ok, 1)
                    v.tensor_tensor(fb_parts[:, 1, :], fb16[:, 0:NE * C], fb_parts[:, 0, :].bitcast(F32), ALU.subtract).then_inc(fb_lo_ok, 1)
                if isinstance(k, int) and k == -1:
                    dve.wait_ge(fb_raw, 1)
                    dve.wait_ge(ld_be, 16)
                    dve.wait_ge(ld_br, 16)
                    v.tensor_tensor(fb16[:, :], fb16[:, :], be16[:, :], ALU.add).then_inc(fb_sb, 1)
                    dve.wait_ge(fb_sb, 1)
                    v.tensor_copy(rb16[:, 3 * C:RB], fb16[:, NE * C:NW]).then_inc(rb_ok, 1)
                    dve.wait_ge(we_hi_ok, 1)
                    v.tensor_tensor(we_lo[:, :], we_t[:, 0:NE * C], we_hi[:, :].bitcast(F32), ALU.subtract)
                    v.tensor_tensor(wr_parts[:, NE:2 * NE], we_t[:, NE * C:NW], wr_parts[:, 0:NE].bitcast(F32), ALU.subtract).then_inc(we_ok, 1)

            steps(dve, step)

        @block.tensor
        def _(pe):
            pe.wait_ge(ident_ok, 1)
            pe.wait_ge(c_silu, 1)
            pe.transpose(work[0][:, 0:NB], c_sb[:, 1, :], ident[0:NB, 0:NB]).then_inc(ct_ps, 1)
            pe.wait_ge(ct_sb, 1)
            pe.wait_ge(ld_mod, 16)
            for j, m in enumerate((0, 1, 3, 4)):
                i = pe.matmul(work[1][:, j * NB:(j + 1) * NB], w_mod_sb[:, m * C:(m + 1) * C], s_t[:, :], start=True, stop=True)
            i.then_inc(mod_ps, 1)

            def three(dst, a_hi, a_lo, b_hi, b_lo):
                pe.matmul(dst, a_hi, b_hi, start=True, stop=False)
                pe.matmul(dst, a_lo, b_hi, start=False, stop=False)
                return pe.matmul(dst, a_hi, b_lo, start=False, stop=True)

            def bias_and_gate_rows():
                pe.wait_ge(mod_sb, 2)
                pe.wait_ge(ld_qkv, 16)
                pe.matmul(att_ps[0:NB, 0:NQKV], shift_col[:, 0, :], wqkv_sb[:, :], start=True, stop=True).then_inc(cb_ps, 1)
                for j, m in enumerate((2, 5)):
                    i = pe.matmul(scores[0:NB, 3, j * C:(j + 1) * C], s_t[:, :], w_mod_sb[:, m * C:(m + 1) * C], start=True, stop=True)
                i.then_inc(gate_ps, 1)

            def expert_weights():
                pe.wait_ge(ld_we, 16)
                pe.wait_ge(ld_wr, 16)
                for e in range(NE):
                    pe.transpose(scores[:, e // 4, (e % 4) * C:(e % 4 + 1) * C], we_sb[:, e, :], ident[:, :])
                pe.transpose(scores[:, 2, 0:NE], wr_sb[:, :], ident[0:NE, 0:NE]).then_inc(wet_ps, 1)

            def expert_bias_rows():
                pe.wait_ge(wet_sb, 1)
                for n, w in enumerate((512, 512, NE)):
                    i = pe.matmul(scores[0:NB, n, 0:w], shift_col[:, 1, :], we_t[:, 512 * n:512 * n + w], start=True, stop=True)
                i.then_inc(fb_ps, 1)

            def warm_up(n, bank):
                for _ in range(n):
                    pe.matmul(bank[:, 0:NQKV], wq_hi[:, 0:P], wq_hi[:, :], start=True, stop=True)

            def qk_scores(k, par, g):
                n = 4 * k + g
                pe.wait_ge(st_sb, 4 * k + g + 1)
                if isinstance(k, int) and k == 0 and g == 0:
                    pe.wait_ge(fb_raw, 1)
                    pe.wait_ge(g_step, 4)
                for half in range(2):
                    if not isinstance(n, int) or n > 0:
                        pe.wait_ge((exp_a, exp_b)[half], n)
                    for t in range(NT):
                        for r in (2 * half, 2 * half + 1):
                            rows = slice(r * ROWS, (r + 1) * ROWS)
                            i = pe.matmul(scores[:, r, t * T:(t + 1) * T], st_t[rows, par, g, t * P:(t + 1) * P],
                                          st_t[rows, par, g, T:2 * T], start=True, stop=True)
                    i.then_inc((qk_a, qk_b)[half], 1)

            def pv(b, q, g):
                pe.wait_ge(exp_a, 4 * b + g + 1)
                pe.wait_ge(exp_b, 4 * b + g + 1)
                if g == 0:
                    pe.wait_ge(qk_sb, NT * (b + 1))
                    if not isinstance(b, int) or b > 0:
                        pe.wait_ge(att_ok, b)
                for t in range(NT):
                    for r in range(R):
                        i = pe.matmul(att_ps[r * ROWS:(r + 1) * ROWS, 0:T], vpad[:, q, t, r, g * ROWS:(g + 1) * ROWS],
                                      probs[:, g, r, t * T:(t + 1) * T], start=(g == 0 and t == 0), stop=(g == G - 1 and t == NT - 1))
                i.then_inc(pv_done, 1)

            def stack(b, g, bank):
                for a, src in enumerate((stk_q, stk_k)):
                    for t in range(NT):
                        heads = src[:, t * H + g * R:t * H + (g + 1) * R, :].rearrange("p r w -> p (r w)")
                        i = pe.transpose(bank[:, a * T + t * P:a * T + (t + 1) * P].bitcast(F32R), heads, ident_r[:, :])
                i.then_inc(st_ps, 1)

            def qkv_tile(t, bank):
                i = three(bank[:, 0:NQKV], h1_hi[:, t * P:(t + 1) * P], h1_lo[:, t * P:(t + 1) * P], wq_hi[:, :], wq_lo[:, :])
                i.then_inc(qkv_ps, 1)

            def expert_chunk(b, q, c, bank):
                for t in range(NT):
                    ts = slice(t * P, (t + 1) * P)
                    ws = slice(c * EC * C, (c + 1) * EC * C)
                    i = three(bank[:, t * EC * C:(t + 1) * EC * C], h2_hi[:, q, ts], h2_lo[:, q, ts], we_hi[:, ws], we_lo[:, ws])
                i.then_inc(f_ps, 1)

            def step(k, par):
                odd = (par + 1) % 2
                a, b, c, router = banks(k)

                alone = isinstance(k, int) and k == NB + 1

                def fill():
                    if isinstance(k, int) and 0 <= k < 2:
                        warm_up(FILL, a)
                    elif isinstance(k, int) and k >= NB and has(k - 2):
                        warm_up(FILL_END, scores[:, R - 1, :] if k == NB else att_ps[:, :])

                if has(k):
                    qk_scores(k, par, 0)
                if has(k):
                    if has(k - 3):
                        pe.wait_ge(acc_step, STEPS * (k - 3) + 3 * STEPS // NC)
                    elif isinstance(k, int) and k == 2:
                        pe.wait_ge(x1_ok, 1)
                    stack(k, 2, b)
                    pe.wait_ge(st_sb, 4 * k + 1)
                    stack(k, 3, c)
                if has(k - 3) and not alone:
                    if has(k):
                        pe.wait_ge(st_sb, 4 * k + 2)
                    elif k == NB:
                        pe.wait_ge(acc_step, STEPS * (k - 3) + 2 * STEPS // NC)
                    expert_chunk(k - 3, odd, 3, a)
                elif has(k):
                    pe.wait_ge(st_sb, 4 * k + 2)
                    fill()
                if has(k - 1):
                    pv(k - 1, odd, 3)
                if has(k - 2):
                    pe.wait_ge(x2n_ok, k - 1)
                    if has(k):
                        pe.wait_ge(st_sb, 4 * k + 3)
                    elif k == NB:
                        pe.wait_ge(acc_step, STEPS * (k - 3) + 3 * STEPS // NC)
                    for t in range(NT):
                        i = pe.transpose(b[:, t * P:(t + 1) * P], x2n[:, par, t * C:(t + 1) * C], ident[:, :])
                    i.then_inc(h2_ps, 1)
                if alone:
                    pe.wait_ge(acc_step, STEPS * (k - 3) + STEPS // NC)
                    expert_chunk(k - 3, odd, 3, work[2])
                if has(k + 1):
                    pe.wait_ge(xn_ok, k + 2)
                    if has(k):
                        pe.wait_ge(st_sb, 4 * k + 4)
                    for t in range(NT):
                        i = pe.transpose(c[:, t * P:(t + 1) * P], xn[:, odd, t * C:(t + 1) * C], ident[:, :])
                    i.then_inc(t1_ps, 1)
                if isinstance(k, int) and k == -1:
                    bias_and_gate_rows()
                    expert_weights()
                fill()
                if has(k):
                    qk_scores(k, par, 1)
                    pv(k, par, 0)
                if has(k - 2):
                    pe.wait_ge(h2_ok, k - 1)
                    if not has(k - 3):
                        pe.wait_ge(we_ok, 1)
                    elif has(k - 1):
                        pe.wait_ge(acc_step, STEPS * (k - 2))
                    for t in range(NT):
                        dst = router[:, 2 * NE * t:2 * NE * (t + 1)]
                        pe.matmul(dst, h2_hi[:, par, t * P:(t + 1) * P], wr_parts[:, :], start=True, stop=False)
                        i = pe.matmul(dst[:, 0:NE], h2_lo[:, par, t * P:(t + 1) * P], wr_parts[:, 0:NE], start=False, stop=True)
                    i.then_inc(r_ps, 1)
                if has(k + 1):
                    pe.wait_ge(t1_ok, k + 2)
                    if isinstance(k, int) and k == -1:
                        pe.wait_ge(wq_ok, 1)
                        pe.wait_ge(ident_r_ok, 1)
                    qkv_tile(0, b)
                    qkv_tile(1, c)
                if has(k):
                    qk_scores(k, par, 2)
                if has(k - 1):
                    pe.wait_ge(att_ok, k)
                    pe.wait_ge(wg_ok, k)
                    if has(k + 1):
                        pe.wait_ge(qk_sb, NT * (k + 1) + 1)
                    for t in range(NT):
                        i = three(b[:, t * C:(t + 1) * C], o_hi[:, t * P:(t + 1) * P], o_lo[:, t * P:(t + 1) * P],
                                  wg_hi[:, odd, :], wg_lo[:, odd, :])
                    i.then_inc(proj_ps, 1)
                if has(k - 2):
                    if has(k + 1):
                        pe.wait_ge(qk_sb, NT * (k + 2))
                    elif has(k):
                        pe.wait_ge(st_sb, 4 * k + 4)
                    expert_chunk(k - 2, par, 0, c)
                    if alone:
                        expert_chunk(k - 2, par, 1, a)
                        expert_chunk(k - 2, par, 2, b)
                    pe.wait_ge(mask_ok, k - 1)
                    for t in range(NT):
                        i = pe.transpose(router[0:2 * NE, T + t * P:T + (t + 1) * P].bitcast(F32R),
                                         mask[:, par, t, :, :].rearrange("p a e -> p (a e)"), ident_r[:, :])
                    i.then_inc(m_ps, 1)
                fill()
                if has(k):
                    pv(k, par, 1)
                if has(k - 2):
                    pe.wait_ge(m_sb, k - 1)
                    pe.wait_ge(fbb_ok, k - 1)
                    for t in range(NT):
                        i = pe.matmul(router[:, t * C:(t + 1) * C], mask_t[:, t * P:(t + 1) * P], fb_b[:, :], start=True, stop=True)
                    i.then_inc(b_ps, 1)
                if has(k):
                    qk_scores(k, par, 3)
                fill()
                if has(k - 2):
                    if not alone:
                        pe.wait_ge(acc_init, k - 1)
                        expert_chunk(k - 2, par, 1, a)
                    if has(k - 1):
                        pe.wait_ge(x1_ok, k)
                    if not alone:
                        expert_chunk(k - 2, par, 2, b)
                if isinstance(k, int) and k == -1:
                    expert_bias_rows()
                    pe.wait_ge(cb_sb, 1)
                    warm_up(WARM, att_ps)
                if has(k + 1):
                    pe.wait_ge(stk_ok, k + 2)
                    if has(k - 2):
                        pe.wait_ge(acc_step, STEPS * (k - 2) + STEPS // NC)
                    stack(k + 1, 0, c)
                if has(k):
                    pv(k, par, 2)
                if has(k + 1):
                    if has(k - 2):
                        pe.wait_ge(acc_step, STEPS * (k - 2) + 2 * STEPS // NC)
                    stack(k + 1, 1, a)
                if isinstance(k, int) and k == -1:
                    warm_up(FILL, att_ps)

            steps(pe, step)


_INS = ['L0_attn_x', 'L0_attn_Wqkv', 'L0_attn_bqkv', 'L0_attn_r_sigma', 'L0_attn_Wproj', 'L0_attn_bproj',
        'L0_ffn_w_router', 'L0_ffn_b_router', 'L0_ffn_w_experts', 'L0_ffn_b_experts', 'L0_c', 'L0_wmod']


def kernel(**inputs):
    import numpy as _np
    import concourse.bacc as _bacc
    from concourse import mybir as _mybir
    from concourse.bass_utils import run_bass_kernel_spmd as _run

    nc = _bacc.Bacc("TRN2", target_bir_lowering=False, num_devices=1)
    arrays, args = {}, []
    for name in _INS:
        a = _np.ascontiguousarray(inputs[name])
        if name == 'L0_attn_r_sigma':
            a = a.reshape(1)
        arrays[f"in_{name}_dram"] = a
        args.append(nc.dram_tensor(f"in_{name}_dram", a.shape, _mybir.dt.from_np(a.dtype), kind="ExternalInput").ap())
    shape = inputs['L0_attn_x'].shape
    args.append(nc.dram_tensor("out_dram", shape, _mybir.dt.float32, kind="ExternalOutput").ap())
    adaln_block(nc, *args)
    r = _run(nc, [arrays], core_ids=[0])
    return r.results[0]["out_dram"]
```
